# Optimizing a Trainium2 kernel written in Bass

```python
import numpy as np
import jax
import jax.numpy as jnp

def _softmax(x, axis=-1):
    return jax.nn.softmax(x, axis=axis)

def _gelu(x):
    return jax.nn.gelu(x, approximate=True)

def _silu(x):
    return jax.nn.silu(x)

def _sigmoid(x):
    return jax.nn.sigmoid(x)

def _layernorm(x, axis=-1, eps=1e-05):
    m = jnp.mean(x, axis=axis, keepdims=True)
    v = jnp.var(x, axis=axis, keepdims=True)
    return (x - m) / jnp.sqrt(v + eps)

def _scatter_add(tgt, idx, src, axis=0):
    return tgt.at[idx].add(src)

def _segment_sum(src, seg, n):
    return jax.ops.segment_sum(src, seg, n)
kernel_name = 'mk_adj_resnorm_d2_adj_r2_0b7c56'

def setup_inputs(seed: int=0):
    np.random.seed(seed)
    _w = jnp.asarray

    def _rec_inputs():
        import jax
        import jax.numpy as jnp
        _gk = jax.random.key(seed)
        x = -0.001547 + 1.001 * jax.random.normal(jax.random.fold_in(_gk, 1), (64, 128, 128), jnp.float32)
        _w = (1.0 + jnp.arange(128, dtype=jnp.float32)) ** (-0.5)
        _w = _w / _w.mean()
        _pij = jnp.clip(0.0625 * _w[:, None] * _w[None, :], 0.0, 1.0)
        _a = jax.random.uniform(jax.random.fold_in(_gk, 2), (64, 128, 128)) < _pij
        _a = jnp.logical_or(_a, jnp.eye(128, dtype=bool))
        adj = _a.astype(jnp.int32)
        _nm = jnp.ones((64, 128), dtype=bool)
        nodemask = jnp.where(_nm, 1.0, 0.0).astype(jnp.float32)
        return (x, adj, nodemask)
    x, adj, nodemask = _rec_inputs()

    def _L0_gnn_setup():
        import jax, jax.numpy as jnp
        import numpy as np
        D_MODEL = 128
        NUM_REL = 40

        def _direction(x, W, Wg, b, bg, adj, rel_ids):
            h = x @ W.T
            g = h @ Wg.T
            vals = (h[:, :, None, :] + b) * jax.nn.sigmoid(g[:, :, None, :] + bg)
            onehot = (adj[..., None] == rel_ids).astype(h.dtype)
            return jnp.einsum('bnmr,bmrd->bnd', onehot, vals)
        key = jax.random.key(seed)
        ks = jax.random.split(key, 16)
        B, N, d = (2, 256, D_MODEL)
        s = 0.02
        inp = {'node': jax.random.normal(ks[0], (B, N, d), dtype=jnp.float32), 'node_mask': jnp.ones((B, N), dtype=jnp.float32), 'adj_mat': jax.random.randint(ks[1], (B, N, N), 0, 41, dtype=jnp.int32), 'W_fwd': jax.random.normal(ks[2], (d, d), dtype=jnp.float32) * s, 'W_bwd': jax.random.normal(ks[3], (d, d), dtype=jnp.float32) * s, 'W_loop': jax.random.normal(ks[4], (d, d), dtype=jnp.float32) * s, 'Wg_fwd': jax.random.normal(ks[5], (d, d), dtype=jnp.float32) * s, 'Wg_bwd': jax.random.normal(ks[6], (d, d), dtype=jnp.float32) * s, 'Wg_loop': jax.random.normal(ks[7], (d, d), dtype=jnp.float32) * s, 'b_fwd': jax.random.normal(ks[8], (NUM_REL - 1, d), dtype=jnp.float32) * s, 'b_bwd': jax.random.normal(ks[9], (NUM_REL - 1, d), dtype=jnp.float32) * s, 'b_loop': jax.random.normal(ks[10], (1, d), dtype=jnp.float32) * s, 'bg_fwd': jax.random.normal(ks[11], (NUM_REL - 1, d), dtype=jnp.float32) * s, 'bg_bwd': jax.random.normal(ks[12], (NUM_REL - 1, d), dtype=jnp.float32) * s, 'bg_loop': jax.random.normal(ks[13], (1, d), dtype=jnp.float32) * s}
        return inp
    _L0_gnn_all = _L0_gnn_setup()
    _L0_gnn_in = {k: v for k, v in _L0_gnn_all.items() if k in ('W_fwd', 'W_bwd', 'W_loop', 'Wg_fwd', 'Wg_bwd', 'Wg_loop', 'b_fwd', 'b_bwd', 'b_loop', 'bg_fwd', 'bg_bwd', 'bg_loop')}
    del _L0_gnn_all

    def _L1_gnn_setup():
        import jax, jax.numpy as jnp
        import numpy as np
        B, N, DIN, DOUT = (16, 512, 128, 128)
        NEG_SLOPE = 0.2
        key = jax.random.key(seed)
        k1, k2, k3, k4 = jax.random.split(key, 4)
        h = jax.random.normal(k1, (B, N, DIN), dtype=jnp.float32)
        adj_mask = jax.random.randint(k2, (B, N, N), 0, 2, dtype=jnp.int32)
        W = jax.random.normal(k3, (DOUT, DIN), dtype=jnp.float32) * (1.0 / np.sqrt(DIN))
        a = jax.random.normal(k4, (2 * DOUT,), dtype=jnp.float32) * (1.0 / np.sqrt(2 * DOUT))
        return {'h': h, 'adj_mask': adj_mask, 'W': W, 'a': a}
    _L1_gnn_all = _L1_gnn_setup()
    _L1_gnn_in = {k: v for k, v in _L1_gnn_all.items() if k in ('W', 'a')}
    del _L1_gnn_all
    return {'x': x, 'adj': adj, 'nodemask': nodemask, 'L0_gnn_W_fwd': _L0_gnn_in['W_fwd'], 'L0_gnn_W_bwd': _L0_gnn_in['W_bwd'], 'L0_gnn_W_loop': _L0_gnn_in['W_loop'], 'L0_gnn_Wg_fwd': _L0_gnn_in['Wg_fwd'], 'L0_gnn_Wg_bwd': _L0_gnn_in['Wg_bwd'], 'L0_gnn_Wg_loop': _L0_gnn_in['Wg_loop'], 'L0_gnn_b_fwd': _L0_gnn_in['b_fwd'], 'L0_gnn_b_bwd': _L0_gnn_in['b_bwd'], 'L0_gnn_b_loop': _L0_gnn_in['b_loop'], 'L0_gnn_bg_fwd': _L0_gnn_in['bg_fwd'], 'L0_gnn_bg_bwd': _L0_gnn_in['bg_bwd'], 'L0_gnn_bg_loop': _L0_gnn_in['bg_loop'], 'L1_gnn_W': _L1_gnn_in['W'], 'L1_gnn_a': _L1_gnn_in['a']}

def reference(x, adj, nodemask, L0_gnn_W_fwd, L0_gnn_W_bwd, L0_gnn_W_loop, L0_gnn_Wg_fwd, L0_gnn_Wg_bwd, L0_gnn_Wg_loop, L0_gnn_b_fwd, L0_gnn_b_bwd, L0_gnn_b_loop, L0_gnn_bg_fwd, L0_gnn_bg_bwd, L0_gnn_bg_loop, L1_gnn_W, L1_gnn_a):
    import jax
    import jax.numpy as jnp

    def _L0_gnn_ref(node, node_mask, adj_mat, W_fwd, W_bwd, W_loop, Wg_fwd, Wg_bwd, Wg_loop, b_fwd, b_bwd, b_loop, bg_fwd, bg_bwd, bg_loop):
        import jax, jax.numpy as jnp
        import numpy as np
        D_MODEL = 128
        NUM_REL = 40

        def _direction(x, W, Wg, b, bg, adj, rel_ids):
            h = x @ W.T
            g = h @ Wg.T
            vals = (h[:, :, None, :] + b) * jax.nn.sigmoid(g[:, :, None, :] + bg)
            onehot = (adj[..., None] == rel_ids).astype(h.dtype)
            return jnp.einsum('bnmr,bmrd->bnd', onehot, vals)
        rels = jnp.arange(2, NUM_REL + 1, dtype=adj_mat.dtype)
        rel1 = jnp.array([1], dtype=adj_mat.dtype)
        adj_t = jnp.swapaxes(adj_mat, -1, -2)
        out = _direction(node, W_fwd, Wg_fwd, b_fwd, bg_fwd, adj_mat, rels)
        out = out + _direction(node, W_bwd, Wg_bwd, b_bwd, bg_bwd, adj_t, rels)
        out = out + _direction(node, W_loop, Wg_loop, b_loop, bg_loop, adj_t, rel1)
        return jax.nn.relu(out)

    def _L1_gnn_ref(h, adj_mask, W, a):
        import jax, jax.numpy as jnp
        import numpy as np
        B, N, DIN, DOUT = (16, 512, 128, 128)
        NEG_SLOPE = 0.2
        Wh = jnp.einsum('bnd,od->bno', h, W)
        d = Wh.shape[-1]
        a1, a2 = (a[:d], a[d:])
        ei = Wh @ a1
        ej = Wh @ a2
        e = ei[:, :, None] + ej[:, None, :]
        e = jnp.where(e > 0, e, NEG_SLOPE * e)
        e = jnp.where(adj_mask == 0, -jnp.inf, e)
        alpha = jax.nn.softmax(e, axis=-1)
        alpha = jnp.where(jnp.isnan(alpha), 0.0, alpha)
        h_out = jnp.einsum('bij,bjo->bio', alpha, Wh)
        return h_out
    x = _layernorm(x + _L0_gnn_ref(x, nodemask, adj, L0_gnn_W_fwd, L0_gnn_W_bwd, L0_gnn_W_loop, L0_gnn_Wg_fwd, L0_gnn_Wg_bwd, L0_gnn_Wg_loop, L0_gnn_b_fwd, L0_gnn_b_bwd, L0_gnn_b_loop, L0_gnn_bg_fwd, L0_gnn_bg_bwd, L0_gnn_bg_loop), axis=-1)
    x = _layernorm(x + _L1_gnn_ref(x, adj, L1_gnn_W, L1_gnn_a), axis=-1)
    return x

_drawn_inputs = setup_inputs


def setup_inputs(seed=0):
    import zlib

    import numpy as np

    out = dict(_drawn_inputs(seed))
    spreads = {}
    factors = {'L0_gnn_Wg_loop': 7.445, 'L0_gnn_bg_loop': 8.0}
    for name, (base, spread) in spreads.items():
        noise = np.random.default_rng([zlib.crc32(name.encode()), seed]).standard_normal(out[name].shape)
        drawn = base * np.exp(spread * noise) if base else spread * noise
        out[name] = jnp.asarray(drawn.astype(out[name].dtype))
    for name, factor in factors.items():
        out[name] = (out[name] * factor).astype(out[name].dtype)
    return out
```

```python
import concourse.bass as bass
from concourse import mybir
from contextlib import ExitStack

F32 = mybir.dt.float32
BF16 = mybir.dt.bfloat16
I32 = mybir.dt.int32
ALU = mybir.AluOpType
ACT = mybir.ActivationFunctionType
X_AXIS = mybir.AxisListType.X

B, N, D = 64, 128, 128
G = 4
GROUPS = B // G
RING = 4
RELATIONS = 39
EPS = 1e-5
SLOPE = 0.2
MASKED = -2.0 ** 126
FLOOR = -1e30
TINY = 1e-30
PARTS = 3
TERMS = PARTS * G * 2


class Group:

    def __init__(self, quad, offset, live=True):
        self.quad, self.offset, self.live = quad, offset, live
        self.slot = offset % RING
        self.half = offset % 2
        self.done = RING * quad + offset + 1
        self.loads = 16 * (quad + offset // RING + 1)
        self.stores = 16 * (2 * quad + offset // 2 + 1)

    def back(self, n):
        return Group(self.quad, self.offset - n)


def steps(engine, quad0, body):

    def step(quad, j, k):
        groups = []
        for age in range(4):
            live = k is None or 0 <= k - age < GROUPS
            groups.append(Group(quad, j - age, live))
        body(*groups)

    for k in range(RING):
        step(quad0, k, k)
    with engine.Fori(quad0 + 1, quad0 + GROUPS // RING) as quad:
        for j in range(RING):
            step(quad, j, None)
    for j in range(3):
        step(quad0 + GROUPS // RING, j, GROUPS + j)


def wait_reuse(engine, semaphore, count):
    if not isinstance(count, int) or count > 0:
        engine.wait_ge(semaphore, count)


def gnn_kernel(nc, x, adj, w_loop, wg_loop, b_loop, bg_loop, w_dir, wg_dir, rel_bias,
               w_att, a_att, identity, selectors, out):
    x_v = x.rearrange("b n d -> n b d")
    adj_v = adj.rearrange("b n m -> n b m")
    out_v = out.rearrange("b n d -> n b d")
    extra_dram = nc.dram_tensor("relation_messages", [N, B, D], F32, kind="Internal").ap()

    ctx = ExitStack()
    with ctx:
        def sb(name, shape, dt=F32):
            return ctx.enter_context(nc.sbuf_tensor(name, shape, dt))

        def sem(name):
            return ctx.enter_context(nc.semaphore(name))

        x_sb = sb("x_sb", [N, RING, G, D])
        adj_sb = sb("adj_sb", [N, RING, G, N], I32)
        extra_sb = sb("extra_sb", [N, RING, G, D])
        xT_sb = sb("xT_sb", [D, 2, G, N])
        gate_sb = sb("gate_sb", [N, 2, G, D])
        vals_sb = sb("vals_sb", [N, 2, G, D])
        one_sb = sb("one_sb", [N, 2, G, N])
        zero_sb = sb("zero_sb", [N, RING, G, N], BF16)
        sum_sb = sb("sum_sb", [N, 2, G, D])
        y_sb = sb("y_sb", [N, 2, G, D])
        stats1 = sb("stats1", [N, 2, G, 6])
        mv1 = sb("mv1", [N, 2, G, 2])
        norm1 = sb("norm1", [N, 2, 3, G])
        x1_sb = sb("x1_sb", [N, RING, G, D])
        x1T_sb = sb("x1T_sb", [D, 2, G, N])
        wh_sb = sb("wh_sb", [N, RING, G, D + 2])
        parts_sb = sb("parts_sb", [N, 2, PARTS, G, 2], BF16)
        rest_sb = sb("rest_sb", [N, 2, G, 2])
        rows_sb = sb("rows_sb", [TERMS, 2, N], BF16)
        slope_sb = sb("slope_sb", [N, 2, G, N])
        logit_sb = sb("logit_sb", [N, 2, G, N])
        rowmax = sb("rowmax", [N, 2, G])
        negmax = sb("negmax", [N, 2, G])
        e_sb = sb("e_sb", [N, 2, G, N])
        rowsum = sb("rowsum", [N, 2, G])
        safesum = sb("safesum", [N, 2, G])
        rinv = sb("rinv", [N, 2, G])
        eT_sb = sb("eT_sb", [N, 2, G, N])
        z_sb = sb("z_sb", [N, 2, G, D])
        stats2 = sb("stats2", [N, 2, G, 6])
        mv2 = sb("mv2", [N, 2, G, 2])
        norm2 = sb("norm2", [N, 2, 3, G])
        out_sb = sb("out_sb", [N, 2, G, D])
        adj_max = sb("adj_max", [N, G, N], I32)
        adj_top = sb("adj_top", [N, 1])
        adj_high = sb("adj_high", [N, 1])
        flag_sb = sb("flag_sb", [1, 1], I32)
        ident = sb("ident", [128, 128])
        ident_bf = sb("ident_bf", [128, 128], BF16)
        masked_ident = sb("masked_ident", [128, 128], BF16)
        sel_f = sb("sel_f", [TERMS, 2, G, N])
        sel = sb("sel", [TERMS, 2, G, N], BF16)
        ones_f = sb("ones_f", [128, 1])
        ones_bf = sb("ones_bf", [128, 128], BF16)
        zeros_f = sb("zeros_f", [128, 128])
        neg_half = sb("neg_half", [N, G])
        eps_sb = sb("eps_sb", [N, G])
        w_in = sb("w_in", [128, 8, 128])
        wgT = sb("wgT", [128, 3, 128])
        whg = sb("whg", [D, 3, 2 * D])
        w1u = sb("w1u", [D, D + 2])
        a_sb = sb("a_sb", [D, 2])
        bias_in = sb("bias_in", [128, 2 * D])
        bias_rest = sb("bias_rest", [128, 2 * D])
        bias_part = sb("bias_part", [128, PARTS, 2 * D], BF16)
        bias_bf = sb("bias_bf", [128, 2, 2 * D], BF16)
        rel_x = sb("rel_x", [N, D])
        rel_adj = sb("rel_adj", [N, N], I32)
        rel_xT = sb("rel_xT", [D, N])
        rel_adjf = sb("rel_adjf", [N, N])
        rel_adjT = sb("rel_adjT", [N, N])
        rel_hg = sb("rel_hg", [N, 2, 2 * D])
        rel_rows = sb("rel_rows", [N, 2, 2 * D])
        rel_pre = sb("rel_pre", [N, 2, 2 * D])
        rel_gate = sb("rel_gate", [N, 2, D])
        rel_mask = sb("rel_mask", [N, 2, N])
        rel_vals = sb("rel_vals", [N, 2, D])
        rel_id = sb("rel_id", [N, 1])
        rel_out = sb("rel_out", [N, D])

        def bank(name, free=(512,), dt=F32):
            return ctx.enter_context(nc.psum_tensor(name, [128, *free], dt))

        ps_t0 = bank("ps_t0", (G, 128))
        ps_t1 = bank("ps_t1", (G, 128))
        ps_hg = [bank(f"ps_hg{i}", (2, 256)) for i in range(2)]
        ps_o = bank("ps_o", (G, 128))
        ps_w0 = bank("ps_w0")
        ps_w1 = bank("ps_w1")
        ps_m = bank("ps_m", (G, 128))
        wh_ps = [t[:, 0:2 * (D + 2)].rearrange("p (b d) -> p b d", b=2) for t in (ps_w0, ps_w1)]
        rows_ps = ps_w0[0:TERMS, 384:448].bitcast(BF16)
        logit_ps = ps_w1[:, :].rearrange("p (b d) -> p b d", b=G)

        s_x = [sem(f"x_in{i}") for i in range(RING)]
        s_adj = [sem(f"adj_in{i}") for i in range(RING)]
        s_extra = [sem(f"extra_in{i}") for i in range(RING)]
        s_stored = [sem(f"stored{i}") for i in range(2)]
        s_weights = sem("weights_in")
        names = ("xT_ready xT_copied hg_ready0 hg_ready1 gate_ready0 gate_ready1 vals_ready masks_ready o_ready "
                 "sum_ready y_ready stats1_ready mv1_ready negmean1_ready var1_ready rstd1_ready x1_ready "
                 "x1T_ready x1T_copied wh_ready0 wh_ready1 wh_copied hi_ready rest_ready mid_ready parts_ready rows_ready "
                 "rows_copied logit_ready slope_ready lrelu_ready rowmax_ready negmax_ready e_ready eT_ready eT_copied m_ready "
                 "safesum_ready rinv_ready z_ready stats2_ready mv2_ready negmean2_ready var2_ready rstd2_ready "
                 "out_ready")
        s = {name: sem(name) for name in names.split()}
        s_const = sem("constants_ready")
        s_setup_pe = sem("setup_products")
        s_setup_dve = sem("setup_copies")
        s_flag = sem("flag_steps")
        s_rel_in, s_rel_rows, s_rel_store = sem("rel_in"), sem("rel_rows_in"), sem("rel_stored")
        s_rel_pe, s_rel_dve, s_rel_act = sem("rel_products"), sem("rel_vector"), sem("rel_gates")

        block = ctx.enter_context(nc.Block())

        N_WEIGHTS = 12
        SETUP_COPIES = 9

        @block.sync
        def _(sp):
            def load(g, first):
                wait_reuse(sp, s["y_ready"], g.back(RING).done)
                wait_reuse(sp, s["masks_ready"], g.back(RING).done)
                at = (G * RING) * (g.quad - first) + G * g.offset
                sp.dma_start(x_sb[:, g.slot], x_v[:, bass.ds(at, G), :]).then_inc(s_x[g.slot], 16)
                sp.dma_start(adj_sb[:, g.slot], adj_v[:, bass.ds(at, G), :]).then_inc(s_adj[g.slot], 16)
                if first:
                    sp.dma_start(extra_sb[:, g.slot], extra_dram[:, bass.ds(at, G), :])\
                        .then_inc(s_extra[g.slot], 16)

            def store(g, first):
                sp.wait_ge(s["out_ready"], g.done)
                at = (G * RING) * (g.quad - first) + G * g.offset
                sp.dma_start(out_v[:, bass.ds(at, G), :], out_sb[:, g.half]).then_inc(s_stored[g.half], 16)

            def run(first):
                load(Group(first, 0), first)
                load(Group(first, 1), first)
                for k in range(RING):
                    load(Group(first, k + 2), first)
                with sp.Fori(first + 1, first + GROUPS // RING - 1) as quad:
                    for j in range(RING):
                        load(Group(quad, j + 2), first)
                        store(Group(quad, j - 4), first)
                last = first + GROUPS // RING - 1
                for j in range(RING):
                    if j < 2:
                        load(Group(last, j + 2), first)
                    store(Group(last, j - 4), first)
                for j in range(RING):
                    store(Group(last, j), first)
                end = Group(last, RING - 1)
                for g in (end.back(1), end):
                    sp.wait_ge(s_stored[g.half], g.stores)

            g0, g1 = Group(0, 0), Group(0, 1)
            sp.dma_start(x_sb[:, 0], x_v[:, 0:G, :]).then_inc(s_x[0], 16)
            sp.dma_start(ident[:, :], identity).then_inc(s_weights, 16)
            for i, w in enumerate((w_loop, wg_loop)):
                sp.dma_start(w_in[:, i, :], w).then_inc(s_weights, 16)
            sp.dma_start(bias_in[:, 0:D], b_loop.broadcast_to([128, D])).then_inc(s_weights, 16)
            sp.dma_start(bias_in[:, D:2 * D], bg_loop.broadcast_to([128, D])).then_inc(s_weights, 16)
            sp.dma_start(adj_sb[:, 0], adj_v[:, 0:G, :]).then_inc(s_adj[0], 16)
            sp.dma_start(w_in[:, 6, :], w_att).then_inc(s_weights, 16)
            sp.dma_start(a_sb[:, :], a_att).then_inc(s_weights, 16)
            sp.dma_start(sel_f[:, :, :, :], selectors.rearrange("r (c b n) -> r c b n", c=2, b=G)).then_inc(s_weights, 16)
            for i in range(2):
                sp.dma_start(w_in[:, 2 + 2 * i, :], w_dir[i]).then_inc(s_weights, 16)
                sp.dma_start(w_in[:, 3 + 2 * i, :], wg_dir[i]).then_inc(s_weights, 16)

            def first_run():
                load(g1, 0)
                for k in range(RING):
                    load(Group(0, k + 2), 0)
                with sp.Fori(1, GROUPS // RING - 1) as quad:
                    for j in range(RING):
                        load(Group(quad, j + 2), 0)
                        store(Group(quad, j - 4), 0)
                last = GROUPS // RING - 1
                for j in range(RING):
                    if j < 2:
                        load(Group(last, j + 2), 0)
                    store(Group(last, j - 4), 0)
                for j in range(RING):
                    store(Group(last, j), 0)
                end = Group(last, RING - 1)
                for g in (end.back(1), end):
                    sp.wait_ge(s_stored[g.half], g.stores)

            first_run()
            sp.wait_ge(s_flag, 4)
            some = sp.value_load(flag_sb[0:1, 0:1], min_val=0, max_val=N)
            with sp.If(some > 0):
                with sp.Fori(0, B) as b:
                    wait_reuse(sp, s_rel_store, 16 * b)
                    sp.dma_start(rel_x[:, :], x_v[:, bass.ds(b, 1), :]).then_inc(s_rel_in, 16)
                    sp.dma_start(rel_adj[:, :], adj_v[:, bass.ds(b, 1), :]).then_inc(s_rel_in, 16)
                    with sp.Fori(0, RELATIONS) as r:
                        sp.wait_ge(s_rel_act, RELATIONS * b + r)
                        sp.wait_ge(s_rel_pe, (RELATIONS + 6) * b + r + 5)
                        sp.dma_start(rel_rows[:, :, :].rearrange("p a d -> p (a d)"),
                                     rel_bias[bass.ds(r, 1), :].broadcast_to([128, 4 * D]))\
                            .then_inc(s_rel_rows, 16)
                    sp.wait_ge(s_rel_dve, (4 + 4 * RELATIONS + 1) * b + 4 + 4 * RELATIONS + 1)
                    sp.dma_start(extra_dram[:, bass.ds(b, 1), :], rel_out[:, :]).then_inc(s_rel_store, 16)
                sp.wait_ge(s_rel_store, 16 * B)
                run(GROUPS // RING)

        @block.tensor
        def _(pe):
            pe.wait_ge(s_weights, 16 * N_WEIGHTS)
            for i in range(3):
                nc.tensor.transpose(ps_t0[:, i, :], w_in[:, 2 * i + 1, :], ident[:, :])
            nc.tensor.transpose(ps_t1[:, 0, :], w_in[:, 0, :], ident[:, :])
            nc.tensor.transpose(ps_t1[:, 1, :], w_in[:, 2, :], ident[:, :])
            nc.tensor.transpose(ps_t1[:, 2, :], w_in[:, 4, :], ident[:, :])
            nc.tensor.transpose(ps_t1[:, 3, :], w_in[:, 6, :], ident[:, :])
            nc.tensor.matmul(ps_m[:, 0, 0:2], w_in[:, 6, :], a_sb[:, :], start=True, stop=True)\
                .then_inc(s_setup_pe, 1)
            pe.wait_ge(s_setup_dve, 1)
            for i in range(3):
                last = nc.tensor.matmul(ps_o[:, i, :], w_in[:, 2 * i, :], wgT[:, i, :], start=True, stop=True)
            last.then_inc(s_setup_pe, 1)
            pe.wait_ge(s_setup_dve, SETUP_COPIES)
            pe.wait_ge(s_const, 3)

            def body(a, b, c, d):
                if a.live:
                    pe.wait_ge(s_x[a.slot], a.loads)
                    wait_reuse(pe, s["x1T_copied"], c.done)
                    for i in range(G):
                        last = nc.tensor.transpose(ps_t0[:, i, :], x_sb[:, a.slot, i, :], ident[:, :])
                    last.then_inc(s["xT_ready"], 1)
                if b.live:
                    pe.wait_ge(s["masks_ready"], b.done)
                    pe.wait_ge(s["vals_ready"], b.done)
                    wait_reuse(pe, s["y_ready"], c.done)
                    for i in range(G):
                        last = nc.tensor.matmul(ps_o[:, i, :], one_sb[:, b.half, i, :], vals_sb[:, b.half, i, :],
                                                start=True, stop=True)
                    last.then_inc(s["o_ready"], 1)
                if c.live:
                    pe.wait_ge(s["parts_ready"], c.done)
                    pe.wait_ge(s["wh_copied"], c.done)
                    nc.tensor.transpose(rows_ps, parts_sb[:, c.half].rearrange("n p b t -> n (p b t)"),
                                        ident_bf[:, :]).then_inc(s["rows_ready"], 1)
                if d.live:
                    pe.wait_ge(s["e_ready"], d.done)
                    wait_reuse(pe, s["eT_copied"], d.back(1).done)
                    for i in range(G):
                        last = nc.tensor.transpose(ps_t1[:, i, :], e_sb[:, d.half, i, :], ident[:, :])
                    last.then_inc(s["eT_ready"], 1)
                if a.live:
                    pe.wait_ge(s["xT_copied"], a.done)
                    wait_reuse(pe, s["vals_ready"], b.done)
                    for p in range(2):
                        nc.tensor.matmul(ps_hg[p][:, :, :], ones_bf[0:96, :], bias_bf[0:96, :, :],
                                         start=True, stop=False)
                        for i in range(2):
                            last = nc.tensor.matmul(ps_hg[p][:, i, :], xT_sb[:, a.half, 2 * p + i, :],
                                                    whg[:, 0, :], start=False, stop=(i == 1))
                        last.then_inc(s[f"hg_ready{p}"], 1)
                if c.live:
                    pe.wait_ge(s["masks_ready"], c.done)
                    pe.wait_ge(s["rows_copied"], c.done)
                    nc.tensor.matmul(logit_ps, masked_ident[:, :], zero_sb[:, c.slot], start=True, stop=False)
                    nc.tensor.matmul(logit_ps, rows_sb[:, c.half, :], sel[:, 0], start=False, stop=False)
                    for i in range(G):
                        last = nc.tensor.matmul(logit_ps[:, i, :], sel[:, 1, i, :], rows_sb[:, c.half, :],
                                                start=False, stop=(i == G - 1))
                    last.then_inc(s["logit_ready"], 1)
                if b.live:
                    pe.wait_ge(s["x1_ready"], b.done)
                    if a.live:
                        pe.wait_ge(s["xT_copied"], a.done)
                    for i in range(G):
                        last = nc.tensor.transpose(ps_t0[:, i, :], x1_sb[:, b.slot, i, :], ident[:, :])
                    last.then_inc(s["x1T_ready"], 1)
                if d.live:
                    pe.wait_ge(s["eT_copied"], d.done)
                    wait_reuse(pe, s["z_ready"], d.back(1).done)
                    for i in range(G):
                        last = nc.tensor.matmul(ps_m[:, i, :], eT_sb[:, d.half, i, :], wh_sb[:, d.slot, i, 0:D],
                                                start=True, stop=True)
                    last.then_inc(s["m_ready"], 1)
                if b.live:
                    pe.wait_ge(s["x1T_copied"], b.done)
                    wait_reuse(pe, s["rows_copied"], c.done)
                    for p in range(2):
                        if p == 1:
                            wait_reuse(pe, s["lrelu_ready"], c.done)
                        for i in range(2):
                            last = nc.tensor.matmul(wh_ps[p][:, i, :], x1T_sb[:, b.half, 2 * p + i, :], w1u[:, :],
                                                    start=True, stop=True)
                        last.then_inc(s[f"wh_ready{p}"], 1)

            steps(pe, 0, body)
            pe.wait_ge(s_flag, 2)
            pe.wait_ge(s["x1T_copied"], GROUPS)
            nc.tensor.matmul(ps_t0[0:1, 0, 0:1], adj_high[:, :], ones_f[:, :], start=True, stop=True)\
                .then_inc(s_flag, 1)
            pe.wait_ge(s_flag, 4)
            some = pe.value_load(flag_sb[0:1, 0:1], min_val=0, max_val=N)
            with pe.If(some > 0):
                PER = RELATIONS + 6
                with pe.Fori(0, B) as b:
                    pe.wait_ge(s_rel_in, 32 * b + 32)
                    if True:
                        nc.tensor.transpose(ps_t0[:, 0, :], rel_x[:, :], ident[:, :]).then_inc(s_rel_pe, 1)
                    pe.wait_ge(s_rel_dve, (5 + 4 * RELATIONS) * b + 2)
                    nc.tensor.transpose(ps_t1[:, 0, :], rel_adjf[:, :], ident[:, :]).then_inc(s_rel_pe, 1)
                    for i in range(2):
                        nc.tensor.matmul(ps_hg[i][:, 0, :], rel_xT[:, :], whg[:, 1 + i, :], start=True, stop=True)\
                            .then_inc(s_rel_pe, 1)
                    nc.tensor.matmul(ps_o[:, 0, :], zeros_f[:, :], zeros_f[:, :], start=True, stop=False)\
                        .then_inc(s_rel_pe, 1)
                    with pe.Fori(0, RELATIONS) as r:
                        pe.wait_ge(s_rel_dve, (5 + 4 * RELATIONS) * b + 4 * r + 8)
                        nc.tensor.matmul(ps_o[:, 0, :], rel_mask[:, 0, :], rel_vals[:, 0, :], start=False, stop=False,
                                         skip_group_check=True)
                        nc.tensor.matmul(ps_o[:, 0, :], rel_mask[:, 1, :], rel_vals[:, 1, :], start=False, stop=False,
                                         skip_group_check=True).then_inc(s_rel_pe, 1)
                    nc.tensor.matmul(ps_o[:, 0, :], zeros_f[:, :], zeros_f[:, :], start=False, stop=True,
                                     skip_group_check=True).then_inc(s_rel_pe, 1)
                    pe.wait_ge(s_rel_dve, (5 + 4 * RELATIONS) * b + 5 + 4 * RELATIONS)
                steps(pe, GROUPS // RING, body)

        @block.scalar
        def _(act):
            def body(a, b, c, d):
                if a.live:
                    act.wait_ge(s["xT_ready"], a.done)
                    wait_reuse(act, s["hg_ready1"], c.done)
                    nc.scalar.copy(xT_sb[:, a.half], ps_t0[:, :, :]).then_inc(s["xT_copied"], 1)
                if c.live:
                    act.wait_ge(s["rows_ready"], c.done)
                    wait_reuse(act, s["logit_ready"], c.back(2).done)
                    nc.scalar.copy(rows_sb[:, c.half, :], rows_ps).then_inc(s["rows_copied"], 1)
                if d.live:
                    act.wait_ge(s["eT_ready"], d.done)
                    wait_reuse(act, s["m_ready"], d.back(2).done)
                    nc.scalar.copy(eT_sb[:, d.half], ps_t1[:, :, :]).then_inc(s["eT_copied"], 1)
                if a.live:
                    wait_reuse(act, s["vals_ready"], c.done)
                    for p in range(2):
                        act.wait_ge(s[f"hg_ready{p}"], a.done)
                        nc.scalar.activation(gate_sb[:, a.half, 2 * p:2 * p + 2, :], ps_hg[p][:, :, D:2 * D],
                                             ACT.Tanh, scale=0.5).then_inc(s[f"gate_ready{p}"], 1)
                if c.live:
                    act.wait_ge(s["logit_ready"], c.done)
                    wait_reuse(act, s["lrelu_ready"], c.back(2).done)
                    nc.scalar.mul(slope_sb[:, c.half], logit_ps, SLOPE).then_inc(s["slope_ready"], 1)
                if b.live:
                    act.wait_ge(s["x1T_ready"], b.done)
                    wait_reuse(act, s["wh_ready1"], b.back(2).done)
                    nc.scalar.copy(x1T_sb[:, b.half], ps_t0[:, :, :]).then_inc(s["x1T_copied"], 1)
                    wait_reuse(act, s["m_ready"], b.back(RING).done)
                    for p in range(2):
                        act.wait_ge(s[f"wh_ready{p}"], b.done)
                        last = nc.scalar.copy(wh_sb[:, b.slot, 2 * p:2 * p + 2, :], wh_ps[p])
                    last.then_inc(s["wh_copied"], 1)
                if c.live:
                    act.wait_ge(s["negmax_ready"], c.done)
                    wait_reuse(act, s["eT_ready"], c.back(2).done)
                    wait_reuse(act, s["rinv_ready"], c.back(2).done)
                    for i in range(G):
                        last = nc.scalar.activation(e_sb[:, c.half, i, :], logit_sb[:, c.half, i, :], ACT.Exp,
                                                    bias=negmax[:, c.half, i:i + 1],
                                                    accum_out=rowsum[:, c.half, i:i + 1])
                    last.then_inc(s["e_ready"], 1)

            steps(act, 0, body)
            act.wait_ge(s_flag, 4)
            some = act.value_load(flag_sb[0:1, 0:1], min_val=0, max_val=N)
            with act.If(some > 0):
                with act.Fori(0, B) as b:
                    with act.Fori(0, RELATIONS) as r:
                        act.wait_ge(s_rel_dve, (5 + 4 * RELATIONS) * b + 4 * r + 6)
                        nc.scalar.activation(rel_gate[:, :, :], rel_pre[:, :, D:2 * D], ACT.Tanh, scale=0.5)\
                            .then_inc(s_rel_act, 1)
                steps(act, GROUPS // RING, body)

        @block.vector
        def _(dve):
            nc.vector.memset(ones_f[:, :], 1.0)
            nc.vector.memset(ones_bf[:, :], 1.0)
            nc.vector.memset(zeros_f[:, :], 0.0).then_inc(s_const, 1)
            nc.vector.memset(bias_bf[:, :, :], 0.0).then_inc(s_const, 1)
            nc.vector.memset(adj_max[:, :, :], 0).then_inc(s_const, 1)
            dve.wait_ge(s_weights, 16 * N_WEIGHTS)
            dve.wait_ge(s_setup_pe, 1)
            nc.vector.tensor_copy(wgT[:, :, :], ps_t0[:, 0:3, :]).then_inc(s_setup_dve, 1)
            nc.vector.tensor_scalar(whg[:, 0, 0:D], ps_t1[:, 0, :], 0.5, None, ALU.mult)
            nc.vector.tensor_copy(whg[:, 1:3, 0:D], ps_t1[:, 1:3, :])
            nc.vector.tensor_copy(w1u[:, 0:D], ps_t1[:, 3, :])
            nc.vector.tensor_copy(w1u[:, D:D + 2], ps_m[:, 0, 0:2])
            nc.vector.tensor_copy(ident_bf[:, :], ident[:, :])
            nc.vector.tensor_scalar(masked_ident[:, :], ident[:, :], MASKED, None, ALU.mult)
            nc.vector.tensor_copy(sel[:, :, :, :], sel_f[:, :, :, :])
            nc.vector.tensor_scalar(bias_in[:, 0:D], bias_in[:, 0:D], 0.5, None, ALU.mult).then_inc(s_setup_dve, 1)
            dve.wait_ge(s_setup_dve, 2)
            nc.vector.tensor_copy(bias_part[:, 0, :], bias_in[:, :]).then_inc(s_setup_dve, 1)
            dve.wait_ge(s_setup_dve, 3)
            nc.vector.tensor_tensor(bias_rest[:, :], bias_in[:, :], bias_part[:, 0, :], ALU.subtract)\
                .then_inc(s_setup_dve, 1)
            dve.wait_ge(s_setup_dve, 4)
            nc.vector.tensor_copy(bias_part[:, 1, :], bias_rest[:, :]).then_inc(s_setup_dve, 1)
            dve.wait_ge(s_setup_dve, 5)
            nc.vector.tensor_tensor(bias_part[:, 2, :], bias_rest[:, :], bias_part[:, 1, :], ALU.subtract)\
                .then_inc(s_setup_dve, 1)
            dve.wait_ge(s_setup_dve, 6)
            dve.wait_ge(s_const, 3)
            for part in range(PARTS):
                row = 32 * part
                for i in range(2):
                    last = nc.vector.tensor_copy(bias_bf[row:row + 1, i, :], bias_part[row:row + 1, part, :])
            last.then_inc(s_setup_dve, 1)
            dve.wait_ge(s_setup_pe, 2)
            nc.vector.tensor_copy(whg[:, :, D:2 * D], ps_o[:, 0:3, :]).then_inc(s_setup_dve, 1)
            nc.vector.memset(rel_id[:, :], 1.0).then_inc(s_setup_dve, 1)

            def body(a, b, c, d, extra=False):
                if c.live:
                    e_cols = wh_sb[:, c.slot, :, D:D + 2]
                    dve.wait_ge(s["wh_copied"], c.done)
                    wait_reuse(dve, s["rows_ready"], c.back(2).done)
                    nc.vector.tensor_copy(parts_sb[:, c.half, 0], e_cols).then_inc(s["hi_ready"], 1)
                    dve.wait_ge(s["hi_ready"], c.done)
                    nc.vector.tensor_tensor(rest_sb[:, c.half], e_cols, parts_sb[:, c.half, 0], ALU.subtract)\
                        .then_inc(s["rest_ready"], 1)
                    dve.wait_ge(s["rest_ready"], c.done)
                    nc.vector.tensor_copy(parts_sb[:, c.half, 1], rest_sb[:, c.half]).then_inc(s["mid_ready"], 1)
                    dve.wait_ge(s["mid_ready"], c.done)
                    nc.vector.tensor_tensor(parts_sb[:, c.half, 2], rest_sb[:, c.half], parts_sb[:, c.half, 1],
                                            ALU.subtract).then_inc(s["parts_ready"], 1)
                if b.live:
                    dve.wait_ge(s["o_ready"], b.done)
                    wait_reuse(dve, s["x1_ready"], b.back(2).done)
                    messages = ps_o[:, :, :]
                    if extra:
                        dve.wait_ge(s_extra[b.slot], b.loads - 16 * (GROUPS // RING))
                        nc.vector.tensor_tensor(sum_sb[:, b.half], ps_o[:, :, :], extra_sb[:, b.slot], ALU.add)\
                            .then_inc(s["sum_ready"], 1)
                        dve.wait_ge(s["sum_ready"], b.done - GROUPS)
                        messages = sum_sb[:, b.half]
                    nc.vector.scalar_tensor_tensor(y_sb[:, b.half], messages, 0.0, x_sb[:, b.slot], ALU.max, ALU.add)\
                        .then_inc(s["y_ready"], 1)
                    dve.wait_ge(s["y_ready"], b.done)
                    for i in range(G):
                        last = nc.vector.bn_stats(stats1[:, b.half, i, :], y_sb[:, b.half, i, :])
                    last.then_inc(s["stats1_ready"], 1)
                    dve.wait_ge(s_const, 3)
                    dve.wait_ge(s["stats1_ready"], b.done)
                    for i in range(G):
                        last = nc.vector.bn_aggr(mv1[:, b.half, i, :], stats1[:, b.half, i, :])
                    last.then_inc(s["mv1_ready"], 1)
                if a.live:
                    dve.wait_ge(s_adj[a.slot], a.loads)
                    wait_reuse(dve, s["o_ready"], c.done)
                    wait_reuse(dve, s["logit_ready"], a.back(RING).done)
                    nc.vector.tensor_tensor(adj_max[:, :, :], adj_max[:, :, :], adj_sb[:, a.slot], ALU.max)
                    nc.vector.tensor_scalar(one_sb[:, a.half], adj_sb[:, a.slot], 1, None, ALU.is_equal)
                    nc.vector.tensor_scalar(zero_sb[:, a.slot], adj_sb[:, a.slot], 0, None, ALU.is_equal)\
                        .then_inc(s["masks_ready"], 1)
                    wait_reuse(dve, s["o_ready"], c.done)
                    for p in range(2):
                        dve.wait_ge(s[f"gate_ready{p}"], a.done)
                        last = nc.vector.scalar_tensor_tensor(
                            vals_sb[:, a.half, 2 * p:2 * p + 2, :], gate_sb[:, a.half, 2 * p:2 * p + 2, :], 1.0,
                            ps_hg[p][:, :, 0:D], ALU.add, ALU.mult)
                    last.then_inc(s["vals_ready"], 1)
                if c.live:
                    dve.wait_ge(s["slope_ready"], c.done)
                    wait_reuse(dve, s["e_ready"], c.back(2).done)
                    nc.vector.tensor_tensor(logit_sb[:, c.half], logit_ps, slope_sb[:, c.half], ALU.max)\
                        .then_inc(s["lrelu_ready"], 1)
                    dve.wait_ge(s["lrelu_ready"], c.done)
                    nc.vector.tensor_reduce(rowmax[:, c.half, :], logit_sb[:, c.half], X_AXIS, ALU.max)\
                        .then_inc(s["rowmax_ready"], 1)
                    dve.wait_ge(s["rowmax_ready"], c.done)
                    nc.vector.tensor_scalar(negmax[:, c.half, :], rowmax[:, c.half, :], FLOOR, -1.0, ALU.max, ALU.mult)\
                        .then_inc(s["negmax_ready"], 1)
                if d.live:
                    dve.wait_ge(s["e_ready"], d.done)
                    nc.vector.tensor_scalar(safesum[:, d.half, :], rowsum[:, d.half, :], TINY, None, ALU.max)\
                        .then_inc(s["safesum_ready"], 1)
                    dve.wait_ge(s["safesum_ready"], d.done)
                    nc.vector.reciprocal(rinv[:, d.half, :], safesum[:, d.half, :]).then_inc(s["rinv_ready"], 1)
                    dve.wait_ge(s["rinv_ready"], d.done)
                    dve.wait_ge(s["m_ready"], d.done)
                    wait_reuse(dve, s["out_ready"], d.back(2).done)
                    for i in range(G):
                        last = nc.vector.scalar_tensor_tensor(z_sb[:, d.half, i, :], ps_m[:, i, :],
                                                              rinv[:, d.half, i:i + 1], x1_sb[:, d.slot, i, :],
                                                              ALU.mult, ALU.add)
                    last.then_inc(s["z_ready"], 1)
                    dve.wait_ge(s["z_ready"], d.done)
                    for i in range(G):
                        last = nc.vector.bn_stats(stats2[:, d.half, i, :], z_sb[:, d.half, i, :])
                    last.then_inc(s["stats2_ready"], 1)
                    dve.wait_ge(s_const, 3)
                    dve.wait_ge(s["stats2_ready"], d.done)
                    for i in range(G):
                        last = nc.vector.bn_aggr(mv2[:, d.half, i, :], stats2[:, d.half, i, :])
                    last.then_inc(s["mv2_ready"], 1)

            steps(dve, 0, body)
            nc.vector.tensor_reduce(adj_top[:, :], adj_max[:, :, :], mybir.AxisListType.XY, ALU.max).then_inc(s_flag, 1)
            dve.wait_ge(s_flag, 1)
            nc.vector.tensor_scalar(adj_high[:, :], adj_top[:, :], 2.0, None, ALU.is_ge).then_inc(s_flag, 1)
            dve.wait_ge(s_flag, 3)
            nc.vector.tensor_copy(flag_sb[:, :], ps_t0[0:1, 0, 0:1]).then_inc(s_flag, 1)
            dve.wait_ge(s_flag, 4)
            some = dve.value_load(flag_sb[0:1, 0:1], min_val=0, max_val=N)
            with dve.If(some > 0):
                PER = 5 + 4 * RELATIONS
                with dve.Fori(0, B) as b:
                    dve.wait_ge(s_rel_pe, (RELATIONS + 6) * b + 1)
                    nc.vector.tensor_copy(rel_xT[:, :], ps_t0[:, 0, :]).then_inc(s_rel_dve, 1)
                    nc.vector.tensor_copy(rel_adjf[:, :], rel_adj[:, :]).then_inc(s_rel_dve, 1)
                    dve.wait_ge(s_rel_pe, (RELATIONS + 6) * b + 4)
                    nc.vector.tensor_copy(rel_adjT[:, :], ps_t1[:, 0, :])
                    nc.vector.tensor_copy(rel_hg[:, 0, :], ps_hg[0][:, 0, :])
                    nc.vector.tensor_copy(rel_hg[:, 1, :], ps_hg[1][:, 0, :]).then_inc(s_rel_dve, 1)
                    nc.vector.memset(rel_id[:, :], 1.0).then_inc(s_rel_dve, 1)
                    with dve.Fori(0, RELATIONS) as r:
                        dve.wait_ge(s_rel_dve, PER * b + 4 * r + 4)
                        nc.vector.tensor_scalar(rel_id[:, :], rel_id[:, :], 1.0, None, ALU.add).then_inc(s_rel_dve, 1)
                        dve.wait_ge(s_rel_rows, 16 * (RELATIONS * b + r) + 16)
                        nc.vector.tensor_tensor(rel_pre[:, :, :], rel_hg[:, :, :], rel_rows[:, :, :], ALU.add)\
                            .then_inc(s_rel_dve, 1)
                        dve.wait_ge(s_rel_dve, PER * b + 4 * r + 6)
                        dve.wait_ge(s_rel_pe, (RELATIONS + 6) * b + r + 5)
                        nc.vector.tensor_scalar(rel_mask[:, 0, :], rel_adjT[:, :], rel_id[:, :], 0.5,
                                                ALU.is_equal, ALU.mult)
                        nc.vector.tensor_scalar(rel_mask[:, 1, :], rel_adjf[:, :], rel_id[:, :], 0.5,
                                                ALU.is_equal, ALU.mult).then_inc(s_rel_dve, 1)
                        dve.wait_ge(s_rel_act, RELATIONS * b + r + 1)
                        nc.vector.scalar_tensor_tensor(rel_vals[:, :, :], rel_gate[:, :, :], 1.0,
                                                       rel_pre[:, :, 0:D], ALU.add, ALU.mult).then_inc(s_rel_dve, 1)
                    dve.wait_ge(s_rel_pe, (RELATIONS + 6) * (b + 1))
                    wait_reuse(dve, s_rel_store, 16 * b)
                    nc.vector.tensor_copy(rel_out[:, :], ps_o[:, 0, :]).then_inc(s_rel_dve, 1)

                def body_extra(a, b, c, d):
                    body(a, b, c, d, extra=True)
                steps(dve, GROUPS // RING, body_extra)

        @block.gpsimd
        def _(pool):
            nc.gpsimd.memset(neg_half[:, :], -0.5).then_inc(s_const, 1)
            nc.gpsimd.memset(eps_sb[:, :], EPS).then_inc(s_const, 1)
            pool.wait_ge(s_const, 5)

            def scale(g, n, mv, norm):
                pool.wait_ge(s[f"mv{n}_ready"], g.done)
                nc.gpsimd.tensor_tensor(norm[:, g.half, 1, :], mv[:, g.half, :, 1], eps_sb[:, :], ALU.add)\
                    .then_inc(s[f"var{n}_ready"], 1)
                nc.gpsimd.tensor_scalar(norm[:, g.half, 0, :], mv[:, g.half, :, 0], -1.0, 1.0, ALU.mult, ALU.mult)\
                    .then_inc(s[f"negmean{n}_ready"], 1)
                pool.wait_ge(s[f"var{n}_ready"], g.done)
                nc.gpsimd.tensor_tensor(norm[:, g.half, 2, :], norm[:, g.half, 1, :], neg_half[:, :], ALU.pow)\
                    .then_inc(s[f"rstd{n}_ready"], 1)
                pool.wait_ge(s_const, 5)
                pool.wait_ge(s[f"rstd{n}_ready"], g.done)
                pool.wait_ge(s[f"negmean{n}_ready"], g.done)

            def body(a, b, c, d):
                if b.live:
                    wait_reuse(pool, s["z_ready"], b.back(RING).done)
                    scale(b, 1, mv1, norm1)
                    for i in range(G):
                        last = nc.gpsimd.tensor_scalar(x1_sb[:, b.slot, i, :], y_sb[:, b.half, i, :],
                                                       norm1[:, b.half, 0, i:i + 1], norm1[:, b.half, 2, i:i + 1],
                                                       ALU.add, ALU.mult)
                    last.then_inc(s["x1_ready"], 1)
                if d.live:
                    wait_reuse(pool, s_stored[d.half], d.back(2).stores)
                    scale(d, 2, mv2, norm2)
                    for i in range(G):
                        last = nc.gpsimd.tensor_scalar(out_sb[:, d.half, i, :], z_sb[:, d.half, i, :],
                                                       norm2[:, d.half, 0, i:i + 1], norm2[:, d.half, 2, i:i + 1],
                                                       ALU.add, ALU.mult)
                    last.then_inc(s["out_ready"], 1)

            steps(pool, 0, body)
            pool.wait_ge(s_flag, 4)
            some = pool.value_load(flag_sb[0:1, 0:1], min_val=0, max_val=N)
            with pool.If(some > 0):
                steps(pool, GROUPS // RING, body)


def kernel(x, adj, nodemask, L0_gnn_W_fwd, L0_gnn_W_bwd, L0_gnn_W_loop, L0_gnn_Wg_fwd, L0_gnn_Wg_bwd,
           L0_gnn_Wg_loop, L0_gnn_b_fwd, L0_gnn_b_bwd, L0_gnn_b_loop, L0_gnn_bg_fwd, L0_gnn_bg_bwd,
           L0_gnn_bg_loop, L1_gnn_W, L1_gnn_a):
    import numpy as np
    import concourse.bacc as bacc
    from concourse.bass_utils import run_bass_kernel_spmd

    selectors = np.zeros((PARTS, G, 2, 2, G, N), np.float32)
    for b in range(G):
        for which in range(2):
            selectors[:, b, which, which, b, :] = 1.0
    arrays = {
        "x": x, "adj": adj, "w_loop": L0_gnn_W_loop, "wg_loop": L0_gnn_Wg_loop,
        "b_loop": L0_gnn_b_loop, "bg_loop": L0_gnn_bg_loop,
        "w_dir": np.stack([np.asarray(L0_gnn_W_fwd), np.asarray(L0_gnn_W_bwd)]),
        "wg_dir": np.stack([np.asarray(L0_gnn_Wg_fwd), np.asarray(L0_gnn_Wg_bwd)]),
        "rel_bias": np.concatenate([np.asarray(t) for t in (L0_gnn_b_fwd, L0_gnn_bg_fwd, L0_gnn_b_bwd,
                                                            L0_gnn_bg_bwd)], axis=1),
        "w_att": L1_gnn_W, "a_att": np.asarray(L1_gnn_a).reshape(2, D).T,
        "identity": np.eye(128, dtype=np.float32),
        "selectors": selectors.reshape(TERMS, 2 * G * N),
    }
    arrays = {name: np.ascontiguousarray(a) for name, a in arrays.items()}
    nc = bacc.Bacc("TRN2", target_bir_lowering=False, num_devices=1)
    ins = [nc.dram_tensor(name, a.shape, mybir.dt.from_np(a.dtype), kind="ExternalInput").ap()
           for name, a in arrays.items()]
    out = nc.dram_tensor("out", (B, N, D), F32, kind="ExternalOutput").ap()
    gnn_kernel(nc, *ins, out)
    r = run_bass_kernel_spmd(nc, [arrays], core_ids=[0])
    return r.results[0]["out"]
```

```python
import concourse.bass as bass
from concourse import mybir
from contextlib import ExitStack

F32 = mybir.dt.float32
BF16 = mybir.dt.bfloat16
I32 = mybir.dt.int32
ALU = mybir.AluOpType
ACT = mybir.ActivationFunctionType
X_AXIS = mybir.AxisListType.X

B, N, D = 64, 128, 128
G = 4
GROUPS = B // G
RING = 4
AGES = 5
RELATIONS = 39
EPS = 1e-5
SLOPE = 0.2
MASKED = -2.0 ** 126
FLOOR = -1e30
TINY = 1e-30
PARTS = 3
TERMS = PARTS * G * 2


class Group:

    def __init__(self, quad, offset, live=True):
        self.quad, self.offset, self.live = quad, offset, live
        self.slot = offset % RING
        self.half = offset % 2
        self.done = RING * quad + offset + 1
        self.loads = 16 * (quad + offset // RING + 1)
        self.stores = 16 * (2 * quad + offset // 2 + 2)

    def back(self, n):
        return Group(self.quad, self.offset - n)


def steps(engine, quad0, body):

    def step(quad, j, k):
        groups = []
        for age in range(AGES):
            live = k is None or 0 <= k - age < GROUPS
            groups.append(Group(quad, j - age, live))
        body(*groups)

    for k in range(RING):
        step(quad0, k, k)
    with engine.Fori(quad0 + 1, quad0 + GROUPS // RING) as quad:
        for j in range(RING):
            step(quad, j, None)
    for j in range(AGES - 1):
        step(quad0 + GROUPS // RING, j, GROUPS + j)


def wait_reuse(engine, semaphore, count):
    if not isinstance(count, int) or count > 0:
        engine.wait_ge(semaphore, count)


def gnn_kernel(nc, x_both, adj, w_loop, wT_loop, wgT_loop, b_loop, bg_loop, w_dir, wT_dir, wgT_dir, rel_bias,
               w_att, wT_att, a_att, identity, selectors, out):
    extra_dram = nc.dram_tensor("relation_messages", [N, B, D], F32, kind="Internal").ap()

    ctx = ExitStack()
    with ctx:
        def sb(name, shape, dt=F32):
            return ctx.enter_context(nc.sbuf_tensor(name, shape, dt))

        def sem(name):
            return ctx.enter_context(nc.semaphore(name))

        x_sb = sb("x_sb", [128, RING, 2, G, 128])
        adj_sb = sb("adj_sb", [N, RING, G, N], I32)
        extra_sb = sb("extra_sb", [N, RING, G, D])
        gate_sb = sb("gate_sb", [N, 2, G, D])
        vals_sb = sb("vals_sb", [N, 2, G, D])
        one_sb = sb("one_sb", [N, 2, G, N])
        zero_sb = sb("zero_sb", [N, RING, G, N], BF16)
        sum_sb = sb("sum_sb", [N, 2, G, D])
        y_sb = sb("y_sb", [N, 2, G, D])
        stats1 = sb("stats1", [N, 2, G, 6])
        mv1 = sb("mv1", [N, 2, G, 2])
        norm1 = sb("norm1", [N, 2, 4, G])
        x1_sb = sb("x1_sb", [N, RING, G, D])
        x1T_sb = sb("x1T_sb", [D, 2, G, N])
        wh_sb = sb("wh_sb", [N, RING, G, D + 2])
        parts_sb = sb("parts_sb", [N, 2, PARTS, G, 2], BF16)
        rest_sb = sb("rest_sb", [N, 2, G, 2])
        rows_sb = sb("rows_sb", [TERMS, 2, N], BF16)
        slope_sb = sb("slope_sb", [N, 2, G, N])
        logit_sb = sb("logit_sb", [N, 2, G, N])
        rowmax = sb("rowmax", [N, 2, G])
        negmax = sb("negmax", [N, 2, G])
        e_sb = sb("e_sb", [N, 2, G, N])
        rowsum = sb("rowsum", [N, 2, G])
        safesum = sb("safesum", [N, 2, G])
        rinv = sb("rinv", [N, 2, G])
        eT_sb = sb("eT_sb", [N, 2, G, N])
        z_sb = sb("z_sb", [N, 2, G, D])
        stats2 = sb("stats2", [N, 2, G, 6])
        mv2 = sb("mv2", [N, 2, G, 2])
        norm2 = sb("norm2", [N, 2, 3, G])
        out_sb = sb("out_sb", [N, 2, G, D])
        adj_over = sb("adj_over", [N, 2, G, N])
        adj_sum = sb("adj_sum", [N, 2])
        adj_total = sb("adj_total", [N, 1])
        adj_high = sb("adj_high", [N, 1])
        flag_sb = sb("flag_sb", [1, 1], I32)
        ident = sb("ident", [128, 128])
        ident_bf = sb("ident_bf", [128, 128], BF16)
        masked_ident = sb("masked_ident", [128, 128], BF16)
        sel_f = sb("sel_f", [TERMS, 2, G, N])
        sel = sb("sel", [TERMS, 2, G, N], BF16)
        ones_f = sb("ones_f", [128, 1])
        ones_bf = sb("ones_bf", [128, 128], BF16)
        zeros_f = sb("zeros_f", [128, 128])
        zero_cols = sb("zero_cols", [N, G, 2])
        neg_one = sb("neg_one", [N, 1])
        neg_half = sb("neg_half", [N, G])
        eps_sb = sb("eps_sb", [N, G])
        w_sb = sb("w_sb", [D, D])
        wgT_sb = sb("wgT_sb", [D, D])
        watt_sb = sb("watt_sb", [D, D])
        whg = sb("whg", [D, 2 * D])
        w1u = sb("w1u", [D, D + 2])
        a_sb = sb("a_sb", [D, 2])
        wdir_sb = sb("wdir_sb", [D, 2, D])
        wgTdir_sb = sb("wgTdir_sb", [D, 2, D])
        whg_dir = sb("whg_dir", [D, 2, 2 * D])
        bias_in = sb("bias_in", [128, 2 * D])
        bias_rest = sb("bias_rest", [128, 2 * D])
        bias_part = sb("bias_part", [128, PARTS, 2 * D], BF16)
        bias_bf = sb("bias_bf", [128, 2, 2 * D], BF16)
        rel_x = sb("rel_x", [N, D])
        rel_adj = sb("rel_adj", [N, N], I32)
        rel_xT = sb("rel_xT", [D, N])
        rel_adjf = sb("rel_adjf", [N, N])
        rel_adjT = sb("rel_adjT", [N, N])
        rel_hg = sb("rel_hg", [N, 2, 2 * D])
        rel_rows = sb("rel_rows", [N, 2, 2 * D])
        rel_pre = sb("rel_pre", [N, 2, 2 * D])
        rel_gate = sb("rel_gate", [N, 2, D])
        rel_mask = sb("rel_mask", [N, 2, N])
        rel_vals = sb("rel_vals", [N, 2, D])
        rel_id = sb("rel_id", [N, 1])
        rel_out = sb("rel_out", [N, D])

        def bank(name, free=(512,), dt=F32):
            return ctx.enter_context(nc.psum_tensor(name, [128, *free], dt))

        ps_t0 = bank("ps_t0", (G, 128))
        ps_t1 = bank("ps_t1", (G, 128))
        ps_hg = [bank(f"ps_hg{i}", (2, 256)) for i in range(2)]
        ps_o = bank("ps_o", (G, 128))
        ps_w0 = bank("ps_w0")
        ps_w1 = bank("ps_w1")
        ps_m = bank("ps_m", (G, 128))
        wh_ps = [t[:, 0:2 * (D + 2)].rearrange("p (b d) -> p b d", b=2) for t in (ps_w0, ps_w1)]
        rows_ps = ps_w0[0:TERMS, 384:448].bitcast(BF16)
        logit_ps = ps_w1[:, :].rearrange("p (b d) -> p b d", b=G)

        s_x = [sem(f"x_in{i}") for i in range(RING)]
        s_adj = [sem(f"adj_in{i}") for i in range(RING)]
        s_extra = [sem(f"extra_in{i}") for i in range(RING)]
        s_stored = [sem(f"stored{i}") for i in range(2)]
        s_w0, s_w1 = sem("loop_weights_in"), sem("loop_biases_in")
        s_w2, s_w3 = sem("attention_weights_in"), sem("identity_in")
        names = ("hg_ready0 hg_ready1 gate_ready0 gate_ready1 vals_ready one_ready zero_ready over_ready total_ready "
                 "o_ready sum_ready y_ready stats1_ready mv1_ready negmean1_ready var1_ready rstd1_ready shift1_ready "
                 "x1_ready x1_ready_too x1T_ready x1T_copied wh_ready0 wh_ready1 wh_copied hi_ready rest_ready mid_ready parts_ready "
                 "rows_ready rows_copied logit_ready slope_ready lrelu_ready rowmax_ready negmax_ready e_ready eT_ready "
                 "eT_copied m_ready safesum_ready rinv_ready z_ready stats2_ready mv2_ready negmean2_ready var2_ready "
                 "rstd2_ready out_ready")
        s = {name: sem(name) for name in names.split()}
        s_const = sem("constants_ready")
        s_setup_pe = sem("setup_products")
        s_setup_dve = sem("setup_copies")
        s_flag = sem("flag_steps")
        s_dir_in, s_dir_pe, s_dir_dve = sem("dir_weights_in"), sem("dir_products"), sem("dir_copies")
        s_rel_in, s_rel_rows, s_rel_store = sem("rel_in"), sem("rel_rows_in"), sem("rel_stored")
        s_rel_pe, s_rel_dve, s_rel_act = sem("rel_products"), sem("rel_vector"), sem("rel_gates")

        REL_PE = RELATIONS + 5
        REL_DVE = 4 * RELATIONS + 4
        SETUP_COPIES = 10

        block = ctx.enter_context(nc.Block())

        @block.sync
        def _(sp):
            QUADS = GROUPS // RING

            def load(g, first):
                wait_reuse(sp, s["vals_ready"], g.back(RING).done)
                wait_reuse(sp, s["y_ready"], g.back(RING).done)
                wait_reuse(sp, s["zero_ready"], g.back(RING).done)
                wait_reuse(sp, s["one_ready"], g.back(RING).done)
                wait_reuse(sp, s["over_ready"], g.back(RING).done)
                at = RING * (g.quad - first) + g.offset
                sp.dma_start(x_sb[:, g.slot].rearrange("p t b n -> p (t b n)"), x_both[:, bass.ds(at, 1), :])\
                    .then_inc(s_x[g.slot], 16)
                sp.dma_start(adj_sb[:, g.slot], adj[:, bass.ds(at * G, G), :]).then_inc(s_adj[g.slot], 16)
                if first:
                    sp.dma_start(extra_sb[:, g.slot], extra_dram[:, bass.ds(at * G, G), :])\
                        .then_inc(s_extra[g.slot], 16)

            def store(g, first):
                at = RING * (g.quad - first) + g.offset
                sp.wait_ge(s["out_ready"], g.done)
                sp.dma_start(out[:, bass.ds(at * G, G), :], out_sb[:, g.half]).then_inc(s_stored[g.half], 16)

            def run(first):
                load(Group(first, 0), first)
                load(Group(first, 1), first)
                for j in range(RING):
                    load(Group(first, j + 2), first)
                with sp.Fori(first + 1, first + QUADS - 1) as quad:
                    for j in range(RING):
                        load(Group(quad, j + 2), first)
                        store(Group(quad, j - RING), first)
                last = first + QUADS - 1
                for j in range(RING):
                    if j < 2:
                        load(Group(last, j + 2), first)
                    store(Group(last, j - RING), first)
                for j in range(RING):
                    store(Group(last, j), first)
                end = Group(last, RING - 1)
                for g in (end.back(1), end):
                    sp.wait_ge(s_stored[g.half], g.stores)

            for half in s_stored:
                sp.sem_inc(half, 16)
            sp.dma_start(w_sb[:, :], w_loop).then_inc(s_w0, 16)
            sp.dma_start(whg[:, 0:D], wT_loop).then_inc(s_w0, 16)
            run(0)
            sp.wait_ge(s_flag, 4)
            some = sp.value_load(flag_sb[0:1, 0:1], min_val=0, max_val=N)
            with sp.If(some > 0):
                sp.dma_start(wdir_sb[:, :, :], w_dir).then_inc(s_dir_in, 16)
                sp.dma_start(wgTdir_sb[:, :, :], wgT_dir).then_inc(s_dir_in, 16)
                sp.dma_start(whg_dir[:, :, 0:D], wT_dir).then_inc(s_dir_in, 16)
                with sp.Fori(0, B) as b:
                    group, graph = b // G, b % G
                    wait_reuse(sp, s_rel_store, 16 * b)
                    sp.dma_start(rel_xT[:, :], x_both[:, bass.ds(group, 1), bass.ds(graph * N + G * D, N)])\
                        .then_inc(s_rel_in, 16)
                    sp.dma_start(rel_adj[:, :], adj[:, bass.ds(b, 1), :]).then_inc(s_rel_in, 16)
                    with sp.Fori(0, RELATIONS) as r:
                        sp.wait_ge(s_rel_act, RELATIONS * b + r)
                        sp.wait_ge(s_rel_pe, REL_PE * b + r + 4)
                        sp.dma_start(rel_rows[:, :, :].rearrange("p a d -> p (a d)"),
                                     rel_bias[bass.ds(r, 1), :].broadcast_to([128, 4 * D]))\
                            .then_inc(s_rel_rows, 16)
                    sp.wait_ge(s_rel_dve, REL_DVE * (b + 1))
                    sp.dma_start(extra_dram[:, bass.ds(b, 1), :], rel_out[:, :]).then_inc(s_rel_store, 16)
                sp.wait_ge(s_rel_store, 16 * B)
                run(QUADS)


        @block.tensor
        def _(pe):
            pe.wait_ge(s_w0, 48)
            nc.tensor.matmul(ps_o[:, 0, :], w_sb[:, :], wgT_sb[:, :], start=True, stop=True).then_inc(s_setup_pe, 1)
            pe.wait_ge(s_w2, 48)
            nc.tensor.matmul(ps_m[:, 0, 0:2], watt_sb[:, :], a_sb[:, :], start=True, stop=True)\
                .then_inc(s_setup_pe, 1)
            pe.wait_ge(s_const, 4)
            pe.wait_ge(s_setup_dve, SETUP_COPIES)
            pe.wait_ge(s_w3, 32)

            def h_g(a, p):
                nc.tensor.matmul(ps_hg[p][:, :, :], ones_bf[0:96, :], bias_bf[0:96, :, :], start=True, stop=False)
                for i in range(2):
                    last = nc.tensor.matmul(ps_hg[p][:, i, :], x_sb[:, a.slot, 1, 2 * p + i, :], whg[:, :],
                                            start=False, stop=(i == 1))
                last.then_inc(s[f"hg_ready{p}"], 1)

            def body(a, b, c, d, e):
                if b.live:
                    pe.wait_ge(s["one_ready"], b.done)
                    pe.wait_ge(s["vals_ready"], b.done)
                    wait_reuse(pe, s["y_ready"], c.done)
                    for i in range(G):
                        last = nc.tensor.matmul(ps_o[:, i, :], one_sb[:, b.half, i, :], vals_sb[:, b.half, i, :],
                                                start=True, stop=True)
                    last.then_inc(s["o_ready"], 1)
                if c.live:
                    pe.wait_ge(s["x1T_copied"], c.done)
                    wait_reuse(pe, s["rows_copied"], d.done)
                    for p in range(2):
                        if p == 1:
                            wait_reuse(pe, s["lrelu_ready"], d.done)
                        for i in range(2):
                            last = nc.tensor.matmul(wh_ps[p][:, i, :], x1T_sb[:, c.half, 2 * p + i, :], w1u[:, :],
                                                    start=True, stop=True)
                        last.then_inc(s[f"wh_ready{p}"], 1)
                if a.live:
                    pe.wait_ge(s_x[a.slot], a.loads)
                    wait_reuse(pe, s["vals_ready"], b.done)
                    h_g(a, 0)
                    h_g(a, 1)
                if c.live:
                    pe.wait_ge(s["parts_ready"], c.done)
                    pe.wait_ge(s["wh_copied"], c.done)
                    nc.tensor.transpose(rows_ps, parts_sb[:, c.half].rearrange("n p b t -> n (p b t)"),
                                        ident_bf[:, :]).then_inc(s["rows_ready"], 1)
                if d.live:
                    pe.wait_ge(s["e_ready"], d.done)
                    wait_reuse(pe, s["eT_copied"], e.done)
                    for i in range(G):
                        last = nc.tensor.transpose(ps_t1[:, i, :], e_sb[:, d.half, i, :], ident[:, :])
                    last.then_inc(s["eT_ready"], 1)
                if c.live:
                    pe.wait_ge(s["zero_ready"], c.done)
                    pe.wait_ge(s["rows_copied"], c.done)
                    nc.tensor.matmul(logit_ps, masked_ident[:, :], zero_sb[:, c.slot], start=True, stop=False)
                    nc.tensor.matmul(logit_ps, rows_sb[:, c.half, :], sel[:, 0], start=False, stop=False)
                    for i in range(G):
                        last = nc.tensor.matmul(logit_ps[:, i, :], sel[:, 1, i, :], rows_sb[:, c.half, :],
                                                start=False, stop=(i == G - 1))
                    last.then_inc(s["logit_ready"], 1)
                if d.live:
                    pe.wait_ge(s["eT_copied"], d.done)
                    wait_reuse(pe, s["z_ready"], e.done)
                    for i in range(G):
                        last = nc.tensor.matmul(ps_m[:, i, :], eT_sb[:, d.half, i, :], wh_sb[:, d.slot, i, 0:D],
                                                start=True, stop=True)
                    last.then_inc(s["m_ready"], 1)
                if b.live:
                    pe.wait_ge(s["x1_ready"], b.done)
                    pe.wait_ge(s["x1_ready_too"], b.done)
                    wait_reuse(pe, s["x1T_copied"], c.done)
                    for i in range(G):
                        last = nc.tensor.transpose(ps_t0[:, i, :], x1_sb[:, b.slot, i, :], ident[:, :])
                    last.then_inc(s["x1T_ready"], 1)

            steps(pe, 0, body)
            pe.wait_ge(s_flag, 2)
            pe.wait_ge(s["x1T_copied"], GROUPS)
            nc.tensor.matmul(ps_t0[0:1, 0, 0:1], adj_high[:, :], ones_f[:, :], start=True, stop=True)\
                .then_inc(s_flag, 1)
            pe.wait_ge(s_flag, 4)
            some = pe.value_load(flag_sb[0:1, 0:1], min_val=0, max_val=N)
            with pe.If(some > 0):
                pe.wait_ge(s_dir_in, 48)
                for i in range(2):
                    last = nc.tensor.matmul(ps_o[:, i, :], wdir_sb[:, i, :], wgTdir_sb[:, i, :], start=True, stop=True)
                last.then_inc(s_dir_pe, 1)
                pe.wait_ge(s_dir_dve, 1)
                with pe.Fori(0, B) as b:
                    pe.wait_ge(s_rel_in, 32 * b + 32)
                    pe.wait_ge(s_rel_dve, REL_DVE * b + 1)
                    nc.tensor.transpose(ps_t1[:, 0, :], rel_adjf[:, :], ident[:, :]).then_inc(s_rel_pe, 1)
                    for i in range(2):
                        nc.tensor.matmul(ps_hg[i][:, 0, :], rel_xT[:, :], whg_dir[:, i, :], start=True, stop=True)\
                            .then_inc(s_rel_pe, 1)
                    nc.tensor.matmul(ps_o[:, 0, :], zeros_f[:, :], zeros_f[:, :], start=True, stop=False)\
                        .then_inc(s_rel_pe, 1)
                    with pe.Fori(0, RELATIONS) as r:
                        pe.wait_ge(s_rel_dve, REL_DVE * b + 4 * r + 7)
                        nc.tensor.matmul(ps_o[:, 0, :], rel_mask[:, 0, :], rel_vals[:, 0, :], start=False, stop=False)
                        nc.tensor.matmul(ps_o[:, 0, :], rel_mask[:, 1, :], rel_vals[:, 1, :], start=False, stop=False)\
                            .then_inc(s_rel_pe, 1)
                    nc.tensor.matmul(ps_o[:, 0, :], zeros_f[:, :], zeros_f[:, :], start=False, stop=True)\
                        .then_inc(s_rel_pe, 1)
                    pe.wait_ge(s_rel_dve, REL_DVE * (b + 1))
                steps(pe, GROUPS // RING, body)

        @block.scalar
        def _(act):
            act.dma_start(wgT_sb[:, :], wgT_loop).then_inc(s_w0, 16)
            act.dma_start(bias_in[:, 0:D], b_loop.broadcast_to([128, D])).then_inc(s_w1, 16)
            act.dma_start(bias_in[:, D:2 * D], bg_loop.broadcast_to([128, D])).then_inc(s_w1, 16)
            act.dma_start(watt_sb[:, :], w_att).then_inc(s_w2, 16)
            act.dma_start(w1u[:, 0:D], wT_att).then_inc(s_w2, 16)
            act.dma_start(a_sb[:, :], a_att).then_inc(s_w2, 16)
            act.dma_start(ident[:, :], identity).then_inc(s_w3, 16)
            act.dma_start(sel_f[:, :, :, :], selectors.rearrange("r (c b n) -> r c b n", c=2, b=G)).then_inc(s_w3, 16)
            act.wait_ge(s_const, 4)

            def body(a, b, c, d, e):
                if a.live:
                    act.wait_ge(s_adj[a.slot], a.loads)
                    wait_reuse(act, s["total_ready"], c.done)
                    nc.scalar.activation(adj_over[:, a.half], adj_sb[:, a.slot], ACT.Relu, bias=neg_one[:, :],
                                         accum_out=adj_sum[:, a.half:a.half + 1]).then_inc(s["over_ready"], 1)
                if c.live:
                    for p in range(2):
                        act.wait_ge(s[f"wh_ready{p}"], c.done)
                        last = nc.scalar.copy(wh_sb[:, c.slot, 2 * p:2 * p + 2, :], wh_ps[p])
                    last.then_inc(s["wh_copied"], 1)
                if d.live:
                    act.wait_ge(s["negmax_ready"], d.done)
                    for i in range(G):
                        last = nc.scalar.activation(e_sb[:, d.half, i, :], logit_sb[:, d.half, i, :], ACT.Exp,
                                                    bias=negmax[:, d.half, i:i + 1],
                                                    accum_out=rowsum[:, d.half, i:i + 1])
                    last.then_inc(s["e_ready"], 1)
                if a.live:
                    wait_reuse(act, s["vals_ready"], c.done)
                    for p in range(2):
                        act.wait_ge(s[f"hg_ready{p}"], a.done)
                        nc.scalar.activation(gate_sb[:, a.half, 2 * p:2 * p + 2, :], ps_hg[p][:, :, D:2 * D],
                                             ACT.Tanh, scale=0.5).then_inc(s[f"gate_ready{p}"], 1)
                if c.live:
                    act.wait_ge(s["rows_ready"], c.done)
                    wait_reuse(act, s["logit_ready"], e.done)
                    nc.scalar.copy(rows_sb[:, c.half, :], rows_ps).then_inc(s["rows_copied"], 1)
                if d.live:
                    act.wait_ge(s["eT_ready"], d.done)
                    nc.scalar.copy(eT_sb[:, d.half], ps_t1[:, :, :]).then_inc(s["eT_copied"], 1)
                if c.live:
                    act.wait_ge(s["logit_ready"], c.done)
                    wait_reuse(act, s["lrelu_ready"], e.done)
                    nc.scalar.mul(slope_sb[:, c.half], logit_ps, SLOPE).then_inc(s["slope_ready"], 1)
                if b.live:
                    act.wait_ge(s["shift1_ready"], b.done)
                    for i in range(2):
                        last = nc.scalar.activation(x1_sb[:, b.slot, i, :], y_sb[:, b.half, i, :], ACT.Identity,
                                                    bias=norm1[:, b.half, 3, i:i + 1],
                                                    scale=norm1[:, b.half, 2, i:i + 1])
                    last.then_inc(s["x1_ready"], 1)
                if b.live:
                    act.wait_ge(s["x1T_ready"], b.done)
                    wait_reuse(act, s["wh_ready1"], b.back(2).done)
                    nc.scalar.copy(x1T_sb[:, b.half], ps_t0[:, :, :]).then_inc(s["x1T_copied"], 1)

            steps(act, 0, body)
            act.wait_ge(s_flag, 4)
            some = act.value_load(flag_sb[0:1, 0:1], min_val=0, max_val=N)
            with act.If(some > 0):
                with act.Fori(0, B) as b:
                    with act.Fori(0, RELATIONS) as r:
                        act.wait_ge(s_rel_dve, REL_DVE * b + 4 * r + 5)
                        nc.scalar.activation(rel_gate[:, :, :], rel_pre[:, :, D:2 * D], ACT.Tanh, scale=0.5)\
                            .then_inc(s_rel_act, 1)
                steps(act, GROUPS // RING, body)


        @block.vector
        def _(dve):
            nc.vector.memset(bias_bf[:, :, :], 0.0).then_inc(s_const, 1)
            nc.vector.memset(ones_bf[:, :], 1.0).then_inc(s_const, 1)
            nc.vector.memset(neg_one[:, :], -1.0).then_inc(s_const, 1)
            dve.wait_ge(s_w1, 32)
            nc.vector.tensor_scalar(bias_in[:, 0:D], bias_in[:, 0:D], 0.5, None, ALU.mult).then_inc(s_setup_dve, 1)
            dve.wait_ge(s_setup_dve, 1)
            nc.vector.tensor_copy(bias_part[:, 0, :], bias_in[:, :]).then_inc(s_setup_dve, 1)
            dve.wait_ge(s_setup_dve, 2)
            nc.vector.tensor_tensor(bias_rest[:, :], bias_in[:, :], bias_part[:, 0, :], ALU.subtract)\
                .then_inc(s_setup_dve, 1)
            dve.wait_ge(s_setup_dve, 3)
            nc.vector.tensor_copy(bias_part[:, 1, :], bias_rest[:, :]).then_inc(s_setup_dve, 1)
            dve.wait_ge(s_setup_dve, 4)
            nc.vector.tensor_tensor(bias_part[:, 2, :], bias_rest[:, :], bias_part[:, 1, :], ALU.subtract)\
                .then_inc(s_setup_dve, 1)
            dve.wait_ge(s_setup_dve, 5)
            dve.wait_ge(s_const, 4)
            for part in range(PARTS):
                row = 32 * part
                for i in range(2):
                    last = nc.vector.tensor_copy(bias_bf[row:row + 1, i, :], bias_part[row:row + 1, part, :])
            last.then_inc(s_setup_dve, 1)
            dve.wait_ge(s_setup_pe, 1)
            nc.vector.tensor_copy(whg[:, D:2 * D], ps_o[:, 0, :]).then_inc(s_setup_dve, 1)
            nc.vector.tensor_scalar(whg[:, 0:D], whg[:, 0:D], 0.5, None, ALU.mult).then_inc(s_setup_dve, 1)
            dve.wait_ge(s_w3, 32)
            nc.vector.tensor_copy(ident_bf[:, :], ident[:, :])
            nc.vector.tensor_scalar(masked_ident[:, :], ident[:, :], MASKED, None, ALU.mult)
            nc.vector.tensor_copy(sel[:, :, :, :], sel_f[:, :, :, :]).then_inc(s_setup_dve, 1)
            dve.wait_ge(s_setup_pe, 2)
            nc.vector.tensor_copy(w1u[:, D:D + 2], ps_m[:, 0, 0:2]).then_inc(s_setup_dve, 1)

            def values(a, p):
                dve.wait_ge(s[f"gate_ready{p}"], a.done)
                return nc.vector.scalar_tensor_tensor(
                    vals_sb[:, a.half, 2 * p:2 * p + 2, :], gate_sb[:, a.half, 2 * p:2 * p + 2, :], 1.0,
                    ps_hg[p][:, :, 0:D], ALU.add, ALU.mult)

            def body(a, b, c, d, e, extra=False):
                if b.live:
                    dve.wait_ge(s["o_ready"], b.done)
                    wait_reuse(dve, s["x1_ready"], b.back(2).done)
                    messages = ps_o[:, :, :]
                    if extra:
                        dve.wait_ge(s_extra[b.slot], b.loads - 16 * (GROUPS // RING))
                        nc.vector.tensor_tensor(sum_sb[:, b.half], ps_o[:, :, :], extra_sb[:, b.slot], ALU.add)\
                            .then_inc(s["sum_ready"], 1)
                        dve.wait_ge(s["sum_ready"], b.done - GROUPS)
                        messages = sum_sb[:, b.half]
                    nc.vector.scalar_tensor_tensor(y_sb[:, b.half], messages, 0.0, x_sb[:, b.slot, 0], ALU.max, ALU.add)\
                        .then_inc(s["y_ready"], 1)
                    dve.wait_ge(s["y_ready"], b.done)
                    for i in range(G):
                        last = nc.vector.bn_stats(stats1[:, b.half, i, :], y_sb[:, b.half, i, :])
                    last.then_inc(s["stats1_ready"], 1)
                if a.live:
                    dve.wait_ge(s_adj[a.slot], a.loads)
                    wait_reuse(dve, s["o_ready"], c.done)
                    nc.vector.tensor_scalar(one_sb[:, a.half], adj_sb[:, a.slot], 1, None, ALU.is_equal)\
                        .then_inc(s["one_ready"], 1)
                if b.live:
                    dve.wait_ge(s_const, 4)
                    dve.wait_ge(s["stats1_ready"], b.done)
                    for i in range(G):
                        last = nc.vector.bn_aggr(mv1[:, b.half, i, :], stats1[:, b.half, i, :])
                    last.then_inc(s["mv1_ready"], 1)
                if e.live:
                    dve.wait_ge(s["z_ready"], e.done)
                    for i in range(G):
                        last = nc.vector.bn_stats(stats2[:, e.half, i, :], z_sb[:, e.half, i, :])
                    last.then_inc(s["stats2_ready"], 1)
                if a.live:
                    values(a, 0)
                    wait_reuse(dve, s["logit_ready"], a.back(RING).done)
                    nc.vector.tensor_scalar(zero_sb[:, a.slot], adj_sb[:, a.slot], 0, None, ALU.is_equal)\
                        .then_inc(s["zero_ready"], 1)
                if e.live:
                    dve.wait_ge(s_const, 4)
                    dve.wait_ge(s["stats2_ready"], e.done)
                    for i in range(G):
                        last = nc.vector.bn_aggr(mv2[:, e.half, i, :], stats2[:, e.half, i, :])
                    last.then_inc(s["mv2_ready"], 1)
                if b.live:
                    dve.wait_ge(s["shift1_ready"], b.done)
                    for i in range(2, G):
                        last = nc.vector.tensor_scalar(x1_sb[:, b.slot, i, :], y_sb[:, b.half, i, :],
                                                       norm1[:, b.half, 2, i:i + 1], norm1[:, b.half, 3, i:i + 1],
                                                       ALU.mult, ALU.add)
                    last.then_inc(s["x1_ready_too"], 1)
                if a.live:
                    values(a, 1).then_inc(s["vals_ready"], 1)
                if d.live:
                    dve.wait_ge(s["e_ready"], d.done)
                    nc.vector.tensor_scalar(safesum[:, d.half, :], rowsum[:, d.half, :], TINY, None, ALU.max)\
                        .then_inc(s["safesum_ready"], 1)
                if c.live:
                    dve.wait_ge(s["slope_ready"], c.done)
                    wait_reuse(dve, s["e_ready"], e.done)
                    nc.vector.tensor_tensor(logit_sb[:, c.half], logit_ps, slope_sb[:, c.half], ALU.max)\
                        .then_inc(s["lrelu_ready"], 1)
                if d.live:
                    dve.wait_ge(s["safesum_ready"], d.done)
                    nc.vector.reciprocal(rinv[:, d.half, :], safesum[:, d.half, :]).then_inc(s["rinv_ready"], 1)
                if c.live:
                    dve.wait_ge(s["lrelu_ready"], c.done)
                    nc.vector.tensor_reduce(rowmax[:, c.half, :], logit_sb[:, c.half], X_AXIS, ALU.max)\
                        .then_inc(s["rowmax_ready"], 1)
                if d.live:
                    dve.wait_ge(s["rinv_ready"], d.done)
                    dve.wait_ge(s["m_ready"], d.done)
                    if not c.live:
                        dve.wait_ge(s["out_ready"], d.back(2).done)
                    for i in range(G):
                        last = nc.vector.scalar_tensor_tensor(z_sb[:, d.half, i, :], ps_m[:, i, :],
                                                              rinv[:, d.half, i:i + 1], x1_sb[:, d.slot, i, :],
                                                              ALU.mult, ALU.add)
                        if i == 0 and c.live:
                            dve.wait_ge(s["rowmax_ready"], c.done)
                            nc.vector.tensor_scalar(negmax[:, c.half, :], rowmax[:, c.half, :], FLOOR, -1.0,
                                                    ALU.max, ALU.mult).then_inc(s["negmax_ready"], 1)
                    last.then_inc(s["z_ready"], 1)
                elif c.live:
                    dve.wait_ge(s["rowmax_ready"], c.done)
                    nc.vector.tensor_scalar(negmax[:, c.half, :], rowmax[:, c.half, :], FLOOR, -1.0,
                                            ALU.max, ALU.mult).then_inc(s["negmax_ready"], 1)

            steps(dve, 0, body)
            dve.wait_ge(s["total_ready"], GROUPS)
            nc.vector.memset(ones_f[:, :], 1.0).then_inc(s_flag, 1)
            nc.vector.tensor_scalar(adj_high[:, :], adj_total[:, :], 0.0, None, ALU.is_gt).then_inc(s_flag, 1)
            dve.wait_ge(s_flag, 3)
            nc.vector.tensor_copy(flag_sb[:, :], ps_t0[0:1, 0, 0:1]).then_inc(s_flag, 1)
            dve.wait_ge(s_flag, 4)
            some = dve.value_load(flag_sb[0:1, 0:1], min_val=0, max_val=N)
            with dve.If(some > 0):
                nc.vector.memset(zeros_f[:, :], 0.0)
                dve.wait_ge(s_dir_pe, 1)
                nc.vector.tensor_copy(whg_dir[:, :, D:2 * D], ps_o[:, 0:2, :]).then_inc(s_dir_dve, 1)
                with dve.Fori(0, B) as b:
                    dve.wait_ge(s_rel_in, 32 * b + 32)
                    nc.vector.tensor_copy(rel_adjf[:, :], rel_adj[:, :]).then_inc(s_rel_dve, 1)
                    dve.wait_ge(s_rel_pe, REL_PE * b + 3)
                    nc.vector.tensor_copy(rel_adjT[:, :], ps_t1[:, 0, :])
                    nc.vector.tensor_copy(rel_hg[:, 0, :], ps_hg[0][:, 0, :])
                    nc.vector.tensor_copy(rel_hg[:, 1, :], ps_hg[1][:, 0, :]).then_inc(s_rel_dve, 1)
                    nc.vector.memset(rel_id[:, :], 1.0).then_inc(s_rel_dve, 1)
                    with dve.Fori(0, RELATIONS) as r:
                        dve.wait_ge(s_rel_dve, REL_DVE * b + 4 * r + 3)
                        nc.vector.tensor_scalar(rel_id[:, :], rel_id[:, :], 1.0, None, ALU.add).then_inc(s_rel_dve, 1)
                        dve.wait_ge(s_rel_rows, 16 * (RELATIONS * b + r) + 16)
                        nc.vector.tensor_tensor(rel_pre[:, :, :], rel_hg[:, :, :], rel_rows[:, :, :], ALU.add)\
                            .then_inc(s_rel_dve, 1)
                        dve.wait_ge(s_rel_dve, REL_DVE * b + 4 * r + 5)
                        dve.wait_ge(s_rel_pe, REL_PE * b + r + 4)
                        nc.vector.tensor_scalar(rel_mask[:, 0, :], rel_adjT[:, :], rel_id[:, :], 0.5,
                                                ALU.is_equal, ALU.mult)
                        nc.vector.tensor_scalar(rel_mask[:, 1, :], rel_adjf[:, :], rel_id[:, :], 0.5,
                                                ALU.is_equal, ALU.mult).then_inc(s_rel_dve, 1)
                        dve.wait_ge(s_rel_act, RELATIONS * b + r + 1)
                        nc.vector.scalar_tensor_tensor(rel_vals[:, :, :], rel_gate[:, :, :], 1.0,
                                                       rel_pre[:, :, 0:D], ALU.add, ALU.mult).then_inc(s_rel_dve, 1)
                    dve.wait_ge(s_rel_pe, REL_PE * (b + 1))
                    wait_reuse(dve, s_rel_store, 16 * b)
                    nc.vector.tensor_copy(rel_out[:, :], ps_o[:, 0, :]).then_inc(s_rel_dve, 1)

                def body_extra(a, b, c, d, e):
                    body(a, b, c, d, e, extra=True)
                steps(dve, GROUPS // RING, body_extra)

        @block.gpsimd
        def _(pool):
            nc.gpsimd.memset(neg_half[:, :], -0.5)
            nc.gpsimd.memset(zero_cols[:, :, :], 0.0)
            nc.gpsimd.memset(adj_total[:, :], 0.0)
            nc.gpsimd.memset(eps_sb[:, :], EPS).then_inc(s_const, 1)
            pool.wait_ge(s_const, 4)

            def scale(g, n, mv, norm):
                pool.wait_ge(s[f"mv{n}_ready"], g.done)
                nc.gpsimd.tensor_tensor(norm[:, g.half, 1, :], mv[:, g.half, :, 1], eps_sb[:, :], ALU.add)\
                    .then_inc(s[f"var{n}_ready"], 1)
                nc.gpsimd.tensor_scalar(norm[:, g.half, 0, :], mv[:, g.half, :, 0], -1.0, 1.0, ALU.mult, ALU.mult)\
                    .then_inc(s[f"negmean{n}_ready"], 1)
                pool.wait_ge(s[f"var{n}_ready"], g.done)
                nc.gpsimd.tensor_tensor(norm[:, g.half, 2, :], norm[:, g.half, 1, :], neg_half[:, :], ALU.pow)\
                    .then_inc(s[f"rstd{n}_ready"], 1)

            def body(a, b, c, d, e):
                if c.live:
                    e_cols = wh_sb[:, c.slot, :, D:D + 2]
                    pool.wait_ge(s["wh_copied"], c.done)
                    wait_reuse(pool, s["rows_ready"], e.done)
                    nc.gpsimd.tensor_tensor(parts_sb[:, c.half, 0], e_cols, zero_cols[:, :, :], ALU.add)\
                        .then_inc(s["hi_ready"], 1)
                    pool.wait_ge(s["hi_ready"], c.done)
                    nc.gpsimd.tensor_tensor(rest_sb[:, c.half], e_cols, parts_sb[:, c.half, 0], ALU.subtract)\
                        .then_inc(s["rest_ready"], 1)
                    pool.wait_ge(s["rest_ready"], c.done)
                    nc.gpsimd.tensor_tensor(parts_sb[:, c.half, 1], rest_sb[:, c.half], zero_cols[:, :, :], ALU.add)\
                        .then_inc(s["mid_ready"], 1)
                    pool.wait_ge(s["mid_ready"], c.done)
                    nc.gpsimd.tensor_tensor(parts_sb[:, c.half, 2], rest_sb[:, c.half], parts_sb[:, c.half, 1],
                                            ALU.subtract).then_inc(s["parts_ready"], 1)
                if b.live:
                    scale(b, 1, mv1, norm1)
                    pool.wait_ge(s["rstd1_ready"], b.done)
                    pool.wait_ge(s["negmean1_ready"], b.done)
                    nc.gpsimd.tensor_tensor(norm1[:, b.half, 3, :], norm1[:, b.half, 2, :], norm1[:, b.half, 0, :],
                                            ALU.mult).then_inc(s["shift1_ready"], 1)
                if a.live:
                    pool.wait_ge(s["over_ready"], a.done)
                    wait_reuse(pool, s["total_ready"], b.done)
                    nc.gpsimd.tensor_tensor(adj_total[:, :], adj_total[:, :], adj_sum[:, a.half:a.half + 1], ALU.add)\
                        .then_inc(s["total_ready"], 1)
                if e.live:
                    pool.wait_ge(s_stored[e.half], e.back(2).stores)
                    scale(e, 2, mv2, norm2)
                    pool.wait_ge(s_const, 4)
                    pool.wait_ge(s["rstd2_ready"], e.done)
                    pool.wait_ge(s["negmean2_ready"], e.done)
                    for i in range(G):
                        last = nc.gpsimd.tensor_scalar(out_sb[:, e.half, i, :], z_sb[:, e.half, i, :],
                                                       norm2[:, e.half, 0, i:i + 1], norm2[:, e.half, 2, i:i + 1],
                                                       ALU.add, ALU.mult)
                    last.then_inc(s["out_ready"], 1)

            steps(pool, 0, body)
            pool.wait_ge(s_flag, 4)
            some = pool.value_load(flag_sb[0:1, 0:1], min_val=0, max_val=N)
            with pool.If(some > 0):
                steps(pool, GROUPS // RING, body)


def kernel(x, adj, nodemask, L0_gnn_W_fwd, L0_gnn_W_bwd, L0_gnn_W_loop, L0_gnn_Wg_fwd, L0_gnn_Wg_bwd,
           L0_gnn_Wg_loop, L0_gnn_b_fwd, L0_gnn_b_bwd, L0_gnn_b_loop, L0_gnn_bg_fwd, L0_gnn_bg_bwd,
           L0_gnn_bg_loop, L1_gnn_W, L1_gnn_a):
    import numpy as np
    import concourse.bacc as bacc
    from concourse.bass_utils import run_bass_kernel_spmd

    selectors = np.zeros((PARTS, G, 2, 2, G, N), np.float32)
    for b in range(G):
        for which in range(2):
            selectors[:, b, which, which, b, :] = 1.0
    grouped = np.asarray(x).reshape(GROUPS, G, N, D)
    x_both = np.stack([grouped.transpose(2, 0, 1, 3), grouped.transpose(3, 0, 1, 2)], axis=2)

    def stacked(fwd, bwd):
        return np.stack([np.asarray(fwd), np.asarray(bwd)], axis=1)

    arrays = {
        "x_both": x_both.reshape(128, GROUPS, 2 * G * 128), "adj": np.asarray(adj).transpose(1, 0, 2),
        "w_loop": L0_gnn_W_loop, "wT_loop": np.asarray(L0_gnn_W_loop).T, "wgT_loop": np.asarray(L0_gnn_Wg_loop).T,
        "b_loop": L0_gnn_b_loop, "bg_loop": L0_gnn_bg_loop,
        "w_dir": stacked(L0_gnn_W_fwd, L0_gnn_W_bwd),
        "wT_dir": stacked(np.asarray(L0_gnn_W_fwd).T, np.asarray(L0_gnn_W_bwd).T),
        "wgT_dir": stacked(np.asarray(L0_gnn_Wg_fwd).T, np.asarray(L0_gnn_Wg_bwd).T),
        "rel_bias": np.concatenate([np.asarray(t) for t in (L0_gnn_b_fwd, L0_gnn_bg_fwd, L0_gnn_b_bwd,
                                                            L0_gnn_bg_bwd)], axis=1),
        "w_att": L1_gnn_W, "wT_att": np.asarray(L1_gnn_W).T, "a_att": np.asarray(L1_gnn_a).reshape(2, D).T,
        "identity": np.eye(128, dtype=np.float32),
        "selectors": selectors.reshape(TERMS, 2 * G * N),
    }
    arrays = {name: np.ascontiguousarray(a) for name, a in arrays.items()}
    nc = bacc.Bacc("TRN2", target_bir_lowering=False, num_devices=1)
    ins = [nc.dram_tensor(name, a.shape, mybir.dt.from_np(a.dtype), kind="ExternalInput").ap()
           for name, a in arrays.items()]
    out = nc.dram_tensor("out", (N, B, D), F32, kind="ExternalOutput").ap()
    gnn_kernel(nc, *ins, out)
    r = run_bass_kernel_spmd(nc, [arrays], core_ids=[0])
    return np.ascontiguousarray(r.results[0]["out"].transpose(1, 0, 2))
```

```python
import concourse.bass as bass
from concourse import mybir
from contextlib import ExitStack

F32 = mybir.dt.float32
BF16 = mybir.dt.bfloat16
I32 = mybir.dt.int32
ALU = mybir.AluOpType
ACT = mybir.ActivationFunctionType
X_AXIS = mybir.AxisListType.X

B, N, D = 64, 128, 128
G = 4
GROUPS = B // G
RING = 4
AGES = 5
RELATIONS = 39
EPS = 1e-5
SLOPE = 0.2
MASKED = -2.0 ** 126
FLOOR = -1e30
WARM_PRODUCTS = (7, 3, 6)
SHARED = 1
PARTS = 3
TERMS = PARTS * G * 2


class Group:

    def __init__(self, quad, offset, live=True):
        self.quad, self.offset, self.live = quad, offset, live
        self.slot = offset % RING
        self.half = offset % 2
        self.done = RING * quad + offset + 1
        self.loads = 16 * (quad + offset // RING + 1)
        self.stores = 16 * (2 * quad + offset // 2 + 2)

    def back(self, n):
        return Group(self.quad, self.offset - n)


def steps(engine, quad0, body, after_first=None):

    def step(quad, j, k):
        groups = []
        for age in range(AGES):
            live = k is None or 0 <= k - age < GROUPS
            groups.append(Group(quad, j - age, live))
        body(*groups)

    for k in range(RING):
        step(quad0, k, k)
        if k == 0 and after_first:
            after_first()
    with engine.Fori(quad0 + 1, quad0 + GROUPS // RING) as quad:
        for j in range(RING):
            step(quad, j, None)
    for j in range(AGES - 1):
        step(quad0 + GROUPS // RING, j, GROUPS + j)


def wait_reuse(engine, semaphore, count):
    if not isinstance(count, int) or count > 0:
        engine.wait_ge(semaphore, count)


def gnn_kernel(nc, x_both, adj, loop_weights, loop_biases, w_dir, wT_dir, wgT_dir, rel_bias, att_weights,
               selectors, out):
    extra_dram = nc.dram_tensor("relation_messages", [N, B, D], F32, kind="Internal").ap()

    ctx = ExitStack()
    with ctx:
        def sb(name, shape, dt=F32):
            return ctx.enter_context(nc.sbuf_tensor(name, shape, dt))

        def sem(name):
            return ctx.enter_context(nc.semaphore(name))

        x_sb = sb("x_sb", [128, RING, 2, G, 128])
        adj_sb = sb("adj_sb", [N, RING, G, N], I32)
        extra_sb = sb("extra_sb", [N, RING, G, D])
        gate_sb = sb("gate_sb", [N, 2, G, D])
        vals_sb = sb("vals_sb", [N, 2, G, D])
        one_sb = sb("one_sb", [N, RING, G, N])
        zero_sb = sb("zero_sb", [N, RING, G, N], BF16)
        sum_sb = sb("sum_sb", [N, 2, G, D])
        y_sb = sb("y_sb", [N, RING, G, D])
        stats1 = sb("stats1", [N, 2, G, 6])
        mv1 = sb("mv1", [N, 2, G, 2])
        norm1 = sb("norm1", [N, RING, 2, G])
        yT_sb = sb("yT_sb", [D, 2, G, N])
        wh_sb = sb("wh_sb", [N, RING, G, D + 2])
        parts_sb = sb("parts_sb", [N, 2, PARTS, G, 2], BF16)
        rest_sb = sb("rest_sb", [N, 2, G, 2])
        rows_sb = sb("rows_sb", [TERMS, 2, N], BF16)
        slope_sb = sb("slope_sb", [N, 2, G, N])
        logit_sb = sb("logit_sb", [N, 2, G, N])
        rowmax = sb("rowmax", [N, 2, G])
        negmax = sb("negmax", [N, 2, G])
        e_sb = sb("e_sb", [N, 2, G, N])
        rowsum = sb("rowsum", [N, 2, G])
        safesum = sb("safesum", [N, 2, G])
        y_scale = sb("y_scale", [N, 2, G])
        eT_sb = sb("eT_sb", [N, 2, G, N])
        z_sb = sb("z_sb", [N, 2, G, D])
        stats2 = sb("stats2", [N, 2, G, 6])
        mv2 = sb("mv2", [N, 2, G, 2])
        norm2 = sb("norm2", [N, 2, 5, G])
        out_sb = sb("out_sb", [N, 2, G, D])
        adj_over = sb("adj_over", [N, 2, G, N])
        adj_sum = sb("adj_sum", [N, 2])
        adj_total = sb("adj_total", [N, 1])
        adj_high = sb("adj_high", [N, 1])
        flag_sb = sb("flag_sb", [1, 1], I32)
        ident_bf = sb("ident_bf", [128, 128], BF16)
        masked_ident = sb("masked_ident", [128, 128], BF16)
        sel_f = sb("sel_f", [TERMS, 2, G, N])
        sel = sb("sel", [TERMS, 2, G, N], BF16)
        ones_f = sb("ones_f", [128, 1])
        ones_bf = sb("ones_bf", [128, 128], BF16)
        zeros_f = sb("zeros_f", [128, 128])
        zero_cols = sb("zero_cols", [N, G, 2])
        neg_one = sb("neg_one", [N, 1])
        act_warm = sb("act_warm", [N, 1])
        neg_half = sb("neg_half", [N, G])
        eps_sb = sb("eps_sb", [N, G])
        loop_in = sb("loop_in", [D, 3 * D])
        whg = sb("whg", [D, 2 * D])
        att_in = sb("att_in", [D, 4 * D + 4])
        w1u = sb("w1u", [D, D + 2])
        wdir_sb = sb("wdir_sb", [D, 2, D])
        wgTdir_sb = sb("wgTdir_sb", [D, 2, D])
        whg_dir = sb("whg_dir", [D, 2, 2 * D])
        bias_in = sb("bias_in", [128, 2 * D])
        bias_rest = sb("bias_rest", [128, 2 * D])
        bias_part = sb("bias_part", [128, PARTS, 2 * D], BF16)
        bias_bf = sb("bias_bf", [128, 2 * D], BF16)
        rel_adj = sb("rel_adj", [N, N], I32)
        rel_xT = sb("rel_xT", [D, N])
        rel_adjf = sb("rel_adjf", [N, N])
        rel_adjT = sb("rel_adjT", [N, N])
        rel_hg = sb("rel_hg", [N, 2, 2 * D])
        rel_rows = sb("rel_rows", [N, 2, 2 * D])
        rel_pre = sb("rel_pre", [N, 2, 2 * D])
        rel_gate = sb("rel_gate", [N, 2, D])
        rel_mask = sb("rel_mask", [N, 2, N])
        rel_vals = sb("rel_vals", [N, 2, D])
        rel_id = sb("rel_id", [N, 1])
        rel_out = sb("rel_out", [N, D])

        w_sb, wgT_sb, wT_sb = (loop_in[:, i * D:(i + 1) * D] for i in range(3))
        ident, centre_sb, watt_sb = (att_in[:, i * D:(i + 1) * D] for i in range(3))
        a_sb = att_in[:, 3 * D:3 * D + 2]
        w1u_raw = att_in[:, 3 * D + 2:4 * D + 4]

        def bank(name, free=(512,), dt=F32):
            return ctx.enter_context(nc.psum_tensor(name, [128, *free], dt))

        ps_t0 = bank("ps_t0", (G, 128))
        ps_t1 = bank("ps_t1", (G, 128))
        ps_hg = [bank(f"ps_hg{i}", (2, 256)) for i in range(2)]
        ps_o = bank("ps_o", (G, 128))
        ps_w0 = bank("ps_w0")
        ps_w1 = bank("ps_w1")
        ps_m = bank("ps_m", (G, 128))
        wh_ps = [t[:, 0:2 * (D + 2)].rearrange("p (b d) -> p b d", b=2) for t in (ps_w0, ps_w1)]
        rows_ps = ps_w0[0:TERMS, 384:448].bitcast(BF16)
        logit_ps = ps_w1[:, :].rearrange("p (b d) -> p b d", b=G)

        s_x = [sem(f"x_in{i}") for i in range(RING)]
        s_adj = [sem(f"adj_in{i}") for i in range(RING)]
        s_extra = [sem(f"extra_in{i}") for i in range(RING)]
        s_stored = [sem(f"stored{i}") for i in range(2)]
        s_w0, s_w1 = sem("loop_weights_in"), sem("loop_biases_in")
        s_w2, s_w3 = sem("attention_weights_in"), sem("selectors_in")
        names = ("hg_ready0 hg_ready1 gate_ready0 gate_ready1 vals0_ready vals_ready one_ready zero_ready "
                 "over_ready total_ready o_ready sum_ready y_ready stats1_ready mv1_ready var1_ready "
                 "rstd1_ready yT_ready yT_copied wh_ready0 wh_ready1 wh_copied hi_ready rest_ready mid_ready "
                 "parts_ready rows_ready rows_copied logit_ready slope_ready lrelu_ready rowmax_ready "
                 "negmax_ready e_ready eT_ready eT_copied m_ready safesum_ready y_scale_ready square_ready "
                 "eps_ready z_ready stats2_ready mv2_ready negmean2_ready var2_ready rstd2_ready out_ready "
                 "out_rest_ready")
        s = {name: sem(name) for name in names.split()}
        s_const = sem("constants_ready")
        s_setup_pe = sem("setup_products")
        s_setup_dve = sem("setup_copies")
        s_flag = sem("flag_steps")
        s_dir_in, s_dir_pe, s_dir_dve = sem("dir_weights_in"), sem("dir_products"), sem("dir_copies")
        s_rel_in, s_rel_rows, s_rel_store = sem("rel_in"), sem("rel_rows_in"), sem("rel_stored")
        s_rel_pe, s_rel_dve, s_rel_act = sem("rel_products"), sem("rel_vector"), sem("rel_gates")

        REL_PE = RELATIONS + 5
        REL_DVE = 4 * RELATIONS + 4
        LOOP_COPIES = 8

        block = ctx.enter_context(nc.Block())

        @block.sync
        def _(sp):
            QUADS = GROUPS // RING

            def load(g, first):
                wait_reuse(sp, s["vals_ready"], g.back(RING).done)
                wait_reuse(sp, s["y_ready"], g.back(RING).done)
                wait_reuse(sp, s["zero_ready"], g.back(RING).done)
                wait_reuse(sp, s["one_ready"], g.back(RING).done)
                wait_reuse(sp, s["over_ready"], g.back(RING).done)
                at = RING * (g.quad - first) + g.offset
                sp.dma_start(x_sb[:, g.slot].rearrange("p t b n -> p (t b n)"), x_both[:, bass.ds(at, 1), :])\
                    .then_inc(s_x[g.slot], 16)
                sp.dma_start(adj_sb[:, g.slot], adj[:, bass.ds(at * G, G), :]).then_inc(s_adj[g.slot], 16)
                if first:
                    sp.dma_start(extra_sb[:, g.slot], extra_dram[:, bass.ds(at * G, G), :])\
                        .then_inc(s_extra[g.slot], 16)

            def store(g, first):
                at = RING * (g.quad - first) + g.offset
                sp.wait_ge(s["out_ready"], g.done)
                sp.dma_start(out[:, bass.ds(at * G, G), :], out_sb[:, g.half]).then_inc(s_stored[g.half], 16)

            def run(first):
                load(Group(first, 0), first)
                load(Group(first, 1), first)
                for j in range(RING):
                    load(Group(first, j + 2), first)
                with sp.Fori(first + 1, first + QUADS - 1) as quad:
                    for j in range(RING):
                        load(Group(quad, j + 2), first)
                        store(Group(quad, j - RING), first)
                last = first + QUADS - 1
                for j in range(RING):
                    if j < 2:
                        load(Group(last, j + 2), first)
                    store(Group(last, j - RING), first)
                end = Group(last, RING - 1)
                for j in range(RING):
                    if j == RING - 1:
                        sp.wait_ge(s["out_rest_ready"], end.done // GROUPS)
                    store(Group(last, j), first)
                for g in (end.back(1), end):
                    sp.wait_ge(s_stored[g.half], g.stores)

            for half in s_stored:
                sp.sem_inc(half, 16)
            sp.dma_start(loop_in[:, :], loop_weights).then_inc(s_w0, 16)
            run(0)
            sp.wait_ge(s_flag, 4)
            some = sp.value_load(flag_sb[0:1, 0:1], min_val=0, max_val=N)
            with sp.If(some > 0):
                sp.dma_start(wdir_sb[:, :, :], w_dir).then_inc(s_dir_in, 16)
                sp.dma_start(wgTdir_sb[:, :, :], wgT_dir).then_inc(s_dir_in, 16)
                sp.dma_start(whg_dir[:, :, 0:D], wT_dir).then_inc(s_dir_in, 16)
                with sp.Fori(0, B) as b:
                    group, graph = b // G, b % G
                    wait_reuse(sp, s_rel_store, 16 * b)
                    sp.dma_start(rel_xT[:, :], x_both[:, bass.ds(group, 1), bass.ds(graph * N + G * D, N)])\
                        .then_inc(s_rel_in, 16)
                    sp.dma_start(rel_adj[:, :], adj[:, bass.ds(b, 1), :]).then_inc(s_rel_in, 16)
                    with sp.Fori(0, RELATIONS) as r:
                        sp.wait_ge(s_rel_act, RELATIONS * b + r)
                        sp.wait_ge(s_rel_pe, REL_PE * b + r + 4)
                        sp.dma_start(rel_rows[:, :, :].rearrange("p a d -> p (a d)"),
                                     rel_bias[bass.ds(r, 1), :].broadcast_to([128, 4 * D]))\
                            .then_inc(s_rel_rows, 16)
                    sp.wait_ge(s_rel_dve, REL_DVE * (b + 1))
                    sp.dma_start(extra_dram[:, bass.ds(b, 1), :], rel_out[:, :]).then_inc(s_rel_store, 16)
                sp.wait_ge(s_rel_store, 16 * B)
                run(QUADS)


        @block.tensor
        def _(pe):
            def warm(products, bank):
                for _ in range(products):
                    nc.tensor.matmul(bank, ones_bf[:, :], ones_bf[:, :].unsqueeze(1).broadcast_to([128, G, 128]),
                                     start=True, stop=True)

            late = ps_hg[1][:, :, :].rearrange("p i (h n) -> p (i h) n", h=2)
            pe.wait_ge(s_const, 4)
            warm(WARM_PRODUCTS[0], ps_m[:, :, :])
            pe.wait_ge(s_w0, 16)
            nc.tensor.matmul(ps_o[:, 0, :], w_sb, wgT_sb, start=True, stop=True).then_inc(s_setup_pe, 1)
            warm(WARM_PRODUCTS[1], ps_m[:, :, :])
            pe.wait_ge(s_w2, 16)
            nc.tensor.matmul(ps_m[:, 0, 0:2], watt_sb, a_sb, start=True, stop=True).then_inc(s_setup_pe, 1)
            pe.wait_ge(s_setup_dve, LOOP_COPIES)

            def attention_weights():
                pe.wait_ge(s_setup_dve, LOOP_COPIES + 2)
                nc.tensor.matmul(ps_m[:, 1:3, :].rearrange("p a b -> p (a b)")[:, 0:D + 2], centre_sb, w1u_raw,
                                 start=True, stop=True).then_inc(s_setup_pe, 1)

            both_biases = bias_bf[0:96, :].unsqueeze(1).broadcast_to([96, 2, 2 * D])

            def h_g(a, p):
                nc.tensor.matmul(ps_hg[p][:, :, :], ones_bf[0:96, :], both_biases, start=True, stop=False)
                for i in range(2):
                    last = nc.tensor.matmul(ps_hg[p][:, i, :], x_sb[:, a.slot, 1, 2 * p + i, :], whg[:, :],
                                            start=False, stop=(i == 1))
                last.then_inc(s[f"hg_ready{p}"], 1)

            def body(a, b, c, d, e):
                if a.live:
                    pe.wait_ge(s_x[a.slot], a.loads)
                    wait_reuse(pe, s["vals0_ready"], b.done)
                    h_g(a, 0)
                if b.live:
                    pe.wait_ge(s["one_ready"], b.done)
                    pe.wait_ge(s["vals_ready"], b.done)
                    wait_reuse(pe, s["y_ready"], c.done)
                    for i in range(G):
                        last = nc.tensor.matmul(ps_o[:, i, :], one_sb[:, b.slot, i, :], vals_sb[:, b.half, i, :],
                                                start=True, stop=True)
                    last.then_inc(s["o_ready"], 1)
                if a.live:
                    h_g(a, 1)
                elif b.live:
                    warm(WARM_PRODUCTS[2], late)
                if c.live:
                    pe.wait_ge(s["parts_ready"], c.done)
                    pe.wait_ge(s["wh_copied"], c.done)
                    nc.tensor.transpose(rows_ps, parts_sb[:, c.half].rearrange("n p b t -> n (p b t)"),
                                        ident_bf[:, :]).then_inc(s["rows_ready"], 1)
                if d.live:
                    pe.wait_ge(s["e_ready"], d.done)
                    wait_reuse(pe, s["eT_copied"], e.done)
                    for i in range(G):
                        last = nc.tensor.transpose(ps_t1[:, i, :], e_sb[:, d.half, i, :], ident)
                    last.then_inc(s["eT_ready"], 1)
                if c.live:
                    pe.wait_ge(s["zero_ready"], c.done)
                    pe.wait_ge(s["rows_copied"], c.done)
                    nc.tensor.matmul(logit_ps, masked_ident[:, :], zero_sb[:, c.slot], start=True, stop=False)
                    nc.tensor.matmul(logit_ps, rows_sb[:, c.half, :], sel[:, 0], start=False, stop=False)
                    for i in range(G):
                        last = nc.tensor.matmul(logit_ps[:, i, :], sel[:, 1, i, :], rows_sb[:, c.half, :],
                                                start=False, stop=(i == G - 1))
                    last.then_inc(s["logit_ready"], 1)
                if b.live:
                    pe.wait_ge(s["y_ready"], b.done)
                    wait_reuse(pe, s["yT_copied"], c.done)
                    for i in range(G):
                        last = nc.tensor.transpose(ps_t0[:, i, :], y_sb[:, b.slot, i, :], ident)
                    last.then_inc(s["yT_ready"], 1)
                if d.live:
                    pe.wait_ge(s["eT_copied"], d.done)
                    wait_reuse(pe, s["z_ready"], e.done)
                    for i in range(G):
                        last = nc.tensor.matmul(ps_m[:, i, :], eT_sb[:, d.half, i, :], wh_sb[:, d.slot, i, 0:D],
                                                start=True, stop=True)
                    last.then_inc(s["m_ready"], 1)
                if b.live:
                    pe.wait_ge(s["yT_copied"], b.done)
                    wait_reuse(pe, s["rows_copied"], c.done)
                    for p in range(2):
                        if p == 1:
                            wait_reuse(pe, s["lrelu_ready"], c.done)
                        for i in range(2):
                            last = nc.tensor.matmul(wh_ps[p][:, i, :], yT_sb[:, b.half, 2 * p + i, :], w1u[:, :],
                                                    start=True, stop=True)
                        last.then_inc(s[f"wh_ready{p}"], 1)
                if c.live and not a.live:
                    warm(WARM_PRODUCTS[2], late)

            steps(pe, 0, body, attention_weights)
            pe.wait_ge(s_flag, 2)
            pe.wait_ge(s["yT_copied"], GROUPS)
            nc.tensor.matmul(ps_t0[0:1, 0, 0:1], adj_high[:, :], ones_f[:, :], start=True, stop=True)\
                .then_inc(s_flag, 1)
            pe.wait_ge(s_flag, 4)
            some = pe.value_load(flag_sb[0:1, 0:1], min_val=0, max_val=N)
            with pe.If(some > 0):
                pe.wait_ge(s_dir_in, 48)
                for i in range(2):
                    last = nc.tensor.matmul(ps_o[:, i, :], wdir_sb[:, i, :], wgTdir_sb[:, i, :], start=True, stop=True)
                last.then_inc(s_dir_pe, 1)
                pe.wait_ge(s_dir_dve, 1)
                with pe.Fori(0, B) as b:
                    pe.wait_ge(s_rel_in, 32 * b + 32)
                    pe.wait_ge(s_rel_dve, REL_DVE * b + 1)
                    nc.tensor.transpose(ps_t1[:, 0, :], rel_adjf[:, :], ident).then_inc(s_rel_pe, 1)
                    for i in range(2):
                        nc.tensor.matmul(ps_hg[i][:, 0, :], rel_xT[:, :], whg_dir[:, i, :], start=True, stop=True)\
                            .then_inc(s_rel_pe, 1)
                    nc.tensor.matmul(ps_o[:, 0, :], zeros_f[:, :], zeros_f[:, :], start=True, stop=False)\
                        .then_inc(s_rel_pe, 1)
                    with pe.Fori(0, RELATIONS) as r:
                        pe.wait_ge(s_rel_dve, REL_DVE * b + 4 * r + 7)
                        nc.tensor.matmul(ps_o[:, 0, :], rel_mask[:, 0, :], rel_vals[:, 0, :], start=False, stop=False)
                        nc.tensor.matmul(ps_o[:, 0, :], rel_mask[:, 1, :], rel_vals[:, 1, :], start=False, stop=False)\
                            .then_inc(s_rel_pe, 1)
                    nc.tensor.matmul(ps_o[:, 0, :], zeros_f[:, :], zeros_f[:, :], start=False, stop=True)\
                        .then_inc(s_rel_pe, 1)
                    pe.wait_ge(s_rel_dve, REL_DVE * (b + 1))
                steps(pe, GROUPS // RING, body)

        @block.scalar
        def _(act):
            act.dma_start(bias_in[:, :], loop_biases.broadcast_to([128, 2 * D])).then_inc(s_w1, 16)
            act.dma_start(att_in[:, 0:4 * D + 2], att_weights).then_inc(s_w2, 16)
            act.dma_start(sel_f[:, :, :, :], selectors.rearrange("r (c b n) -> r c b n", c=2, b=G)).then_inc(s_w3, 16)
            act.wait_ge(s_const, 4)
            nc.scalar.activation(act_warm[:, :], neg_one[:, :], ACT.Tanh, scale=0.5)

            def gates(a, p):
                act.wait_ge(s[f"hg_ready{p}"], a.done)
                nc.scalar.activation(gate_sb[:, a.half, 2 * p:2 * p + 2, :], ps_hg[p][:, :, D:2 * D],
                                     ACT.Tanh, scale=0.5).then_inc(s[f"gate_ready{p}"], 1)

            def body(a, b, c, d, e):
                if d.live:
                    act.wait_ge(s["negmax_ready"], d.done)
                    for i in range(G):
                        last = nc.scalar.activation(e_sb[:, d.half, i, :], logit_sb[:, d.half, i, :], ACT.Exp,
                                                    bias=negmax[:, d.half, i:i + 1],
                                                    accum_out=rowsum[:, d.half, i:i + 1])
                    last.then_inc(s["e_ready"], 1)
                if a.live:
                    wait_reuse(act, s["vals_ready"], c.done)
                    gates(a, 0)
                if c.live:
                    act.wait_ge(s["rows_ready"], c.done)
                    wait_reuse(act, s["logit_ready"], e.done)
                    nc.scalar.copy(rows_sb[:, c.half, :], rows_ps).then_inc(s["rows_copied"], 1)
                if a.live:
                    gates(a, 1)
                if d.live:
                    act.wait_ge(s["eT_ready"], d.done)
                    nc.scalar.copy(eT_sb[:, d.half], ps_t1[:, :, :]).then_inc(s["eT_copied"], 1)
                if c.live:
                    act.wait_ge(s["logit_ready"], c.done)
                    wait_reuse(act, s["lrelu_ready"], e.done)
                    nc.scalar.mul(slope_sb[:, c.half], logit_ps, SLOPE).then_inc(s["slope_ready"], 1)
                if b.live:
                    act.wait_ge(s["yT_ready"], b.done)
                    wait_reuse(act, s["wh_ready1"], b.back(2).done)
                    nc.scalar.copy(yT_sb[:, b.half], ps_t0[:, :, :]).then_inc(s["yT_copied"], 1)
                if a.live:
                    act.wait_ge(s_adj[a.slot], a.loads)
                    wait_reuse(act, s["total_ready"], c.done)
                    nc.scalar.activation(adj_over[:, a.half], adj_sb[:, a.slot], ACT.Relu, bias=neg_one[:, :],
                                         accum_out=adj_sum[:, a.half:a.half + 1]).then_inc(s["over_ready"], 1)
                if b.live:
                    act.wait_ge(s["rstd1_ready"], b.done)
                    for i in range(G):
                        if i % 2 == 0:
                            act.wait_ge(s[f"wh_ready{i // 2}"], b.done)
                        last = nc.scalar.mul(wh_sb[:, b.slot, i, :], wh_ps[i // 2][:, i % 2, :],
                                             norm1[:, b.slot, 1, i:i + 1])
                    last.then_inc(s["wh_copied"], 1)

            steps(act, 0, body)
            act.wait_ge(s_flag, 4)
            some = act.value_load(flag_sb[0:1, 0:1], min_val=0, max_val=N)
            with act.If(some > 0):
                with act.Fori(0, B) as b:
                    with act.Fori(0, RELATIONS) as r:
                        act.wait_ge(s_rel_dve, REL_DVE * b + 4 * r + 5)
                        nc.scalar.activation(rel_gate[:, :, :], rel_pre[:, :, D:2 * D], ACT.Tanh, scale=0.5)\
                            .then_inc(s_rel_act, 1)
                steps(act, GROUPS // RING, body)


        @block.vector
        def _(dve):
            nc.vector.memset(bias_bf[:, :], 0.0).then_inc(s_const, 1)
            nc.vector.memset(ones_bf[:, :], 1.0).then_inc(s_const, 1)
            nc.vector.memset(neg_one[:, :], -1.0).then_inc(s_const, 1)
            dve.wait_ge(s_w1, 16)
            nc.vector.tensor_scalar(bias_in[:, 0:D], bias_in[:, 0:D], 0.5, None, ALU.mult).then_inc(s_setup_dve, 1)
            dve.wait_ge(s_setup_dve, 1)
            nc.vector.tensor_copy(bias_part[:, 0, :], bias_in[:, :]).then_inc(s_setup_dve, 1)
            dve.wait_ge(s_setup_dve, 2)
            nc.vector.tensor_tensor(bias_rest[:, :], bias_in[:, :], bias_part[:, 0, :], ALU.subtract)\
                .then_inc(s_setup_dve, 1)
            dve.wait_ge(s_setup_dve, 3)
            nc.vector.tensor_copy(bias_part[:, 1, :], bias_rest[:, :]).then_inc(s_setup_dve, 1)
            dve.wait_ge(s_setup_dve, 4)
            nc.vector.tensor_tensor(bias_part[:, 2, :], bias_rest[:, :], bias_part[:, 1, :], ALU.subtract)\
                .then_inc(s_setup_dve, 1)
            dve.wait_ge(s_setup_dve, 5)
            dve.wait_ge(s_const, 4)
            for part in range(PARTS):
                row = 32 * part
                last = nc.vector.tensor_copy(bias_bf[row:row + 1, :], bias_part[row:row + 1, part, :])
            last.then_inc(s_setup_dve, 1)
            dve.wait_ge(s_w0, 16)
            nc.vector.tensor_scalar(whg[:, 0:D], wT_sb, 0.5, None, ALU.mult).then_inc(s_setup_dve, 1)
            dve.wait_ge(s_setup_pe, 1)
            nc.vector.tensor_copy(whg[:, D:2 * D], ps_o[:, 0, :]).then_inc(s_setup_dve, 1)

            dve.wait_ge(s_w2, 16)
            nc.vector.tensor_copy(ident_bf[:, :], ident)
            nc.vector.tensor_scalar(masked_ident[:, :], ident, MASKED, None, ALU.mult)
            dve.wait_ge(s_w3, 16)
            nc.vector.tensor_copy(sel[:, :, :, :], sel_f[:, :, :, :]).then_inc(s_setup_dve, 1)
            dve.wait_ge(s_setup_pe, 2)
            nc.vector.tensor_copy(w1u_raw[:, D:D + 2], ps_m[:, 0, 0:2]).then_inc(s_setup_dve, 1)

            def attention_weights():
                dve.wait_ge(s_setup_pe, 3)
                nc.vector.tensor_copy(w1u[:, :], ps_m[:, 1:3, :].rearrange("p a b -> p (a b)")[:, 0:D + 2])\
                    .then_inc(s_setup_dve, 1)

            def values(a, p):
                dve.wait_ge(s[f"gate_ready{p}"], a.done)
                return nc.vector.scalar_tensor_tensor(
                    vals_sb[:, a.half, 2 * p:2 * p + 2, :], gate_sb[:, a.half, 2 * p:2 * p + 2, :], 1.0,
                    ps_hg[p][:, :, 0:D], ALU.add, ALU.mult)

            def body(a, b, c, d, e, extra=False):
                if a.live:
                    dve.wait_ge(s_adj[a.slot], a.loads)
                    wait_reuse(dve, s["o_ready"], a.back(RING).done)
                    nc.vector.tensor_scalar(one_sb[:, a.slot], adj_sb[:, a.slot], 1, None, ALU.is_equal)\
                        .then_inc(s["one_ready"], 1)
                if e.live:
                    dve.wait_ge(s_const, 4)
                    dve.wait_ge(s["stats2_ready"], e.done)
                    for i in range(G):
                        last = nc.vector.bn_aggr(mv2[:, e.half, i, :], stats2[:, e.half, i, :])
                    last.then_inc(s["mv2_ready"], 1)
                if b.live:
                    dve.wait_ge(s["o_ready"], b.done)
                    messages = ps_o[:, :, :]
                    if extra:
                        dve.wait_ge(s_extra[b.slot], b.loads - 16 * (GROUPS // RING))
                        nc.vector.tensor_tensor(sum_sb[:, b.half], ps_o[:, :, :], extra_sb[:, b.slot], ALU.add)\
                            .then_inc(s["sum_ready"], 1)
                        dve.wait_ge(s["sum_ready"], b.done - GROUPS)
                        messages = sum_sb[:, b.half]
                    nc.vector.scalar_tensor_tensor(y_sb[:, b.slot], messages, 0.0, x_sb[:, b.slot, 0], ALU.max, ALU.add)\
                        .then_inc(s["y_ready"], 1)
                if a.live:
                    values(a, 0).then_inc(s["vals0_ready"], 1)
                if b.live:
                    dve.wait_ge(s["y_ready"], b.done)
                    for i in range(G):
                        last = nc.vector.bn_stats(stats1[:, b.half, i, :], y_sb[:, b.slot, i, :])
                    last.then_inc(s["stats1_ready"], 1)
                if a.live:
                    values(a, 1).then_inc(s["vals_ready"], 1)
                if b.live:
                    dve.wait_ge(s_const, 4)
                    dve.wait_ge(s["stats1_ready"], b.done)
                    for i in range(G):
                        last = nc.vector.bn_aggr(mv1[:, b.half, i, :], stats1[:, b.half, i, :])
                    last.then_inc(s["mv1_ready"], 1)
                if c.live:
                    dve.wait_ge(s["slope_ready"], c.done)
                    wait_reuse(dve, s["e_ready"], e.done)
                    nc.vector.tensor_tensor(logit_sb[:, c.half], logit_ps, slope_sb[:, c.half], ALU.max)\
                        .then_inc(s["lrelu_ready"], 1)
                if d.live:
                    dve.wait_ge(s["e_ready"], d.done)
                    if not c.live:
                        dve.wait_ge(s["square_ready"], d.back(2).done)
                    nc.vector.tensor_scalar(safesum[:, d.half, :], rowsum[:, d.half, :], 0.5, None, ALU.max)\
                        .then_inc(s["safesum_ready"], 1)
                if c.live:
                    dve.wait_ge(s["lrelu_ready"], c.done)
                    nc.vector.tensor_reduce(rowmax[:, c.half, :], logit_sb[:, c.half], X_AXIS, ALU.max)\
                        .then_inc(s["rowmax_ready"], 1)
                if d.live:
                    dve.wait_ge(s["safesum_ready"], d.done)
                    dve.wait_ge(s["rstd1_ready"], d.done)
                    nc.vector.tensor_tensor(y_scale[:, d.half, :], safesum[:, d.half, :], norm1[:, d.slot, 1, :], ALU.mult)\
                        .then_inc(s["y_scale_ready"], 1)
                if c.live:
                    dve.wait_ge(s["rowmax_ready"], c.done)
                    nc.vector.tensor_scalar(negmax[:, c.half, :], rowmax[:, c.half, :], FLOOR, -1.0,
                                            ALU.max, ALU.mult).then_inc(s["negmax_ready"], 1)
                if d.live:
                    dve.wait_ge(s["y_scale_ready"], d.done)
                    dve.wait_ge(s["m_ready"], d.done)
                    if not c.live:
                        dve.wait_ge(s["out_ready"], d.back(2).done)
                    for i in range(G):
                        last = nc.vector.scalar_tensor_tensor(z_sb[:, d.half, i, :], y_sb[:, d.slot, i, :],
                                                              y_scale[:, d.half, i:i + 1], ps_m[:, i, :],
                                                              ALU.mult, ALU.add)
                    last.then_inc(s["z_ready"], 1)
                if a.live:
                    wait_reuse(dve, s["logit_ready"], a.back(RING).done)
                    nc.vector.tensor_scalar(zero_sb[:, a.slot], adj_sb[:, a.slot], 0, None, ALU.is_equal)\
                        .then_inc(s["zero_ready"], 1)
                if d.live:
                    dve.wait_ge(s["z_ready"], d.done)
                    for i in range(G):
                        last = nc.vector.bn_stats(stats2[:, d.half, i, :], z_sb[:, d.half, i, :])
                    last.then_inc(s["stats2_ready"], 1)
                if e.live and not d.live:
                    dve.wait_ge(s_const, 4)
                    dve.wait_ge(s_stored[e.half], e.back(2).stores)
                    dve.wait_ge(s["negmean2_ready"], e.done)
                    dve.wait_ge(s["rstd2_ready"], e.done)
                    for i in range(SHARED, G):
                        last = nc.vector.tensor_scalar(out_sb[:, e.half, i, :], z_sb[:, e.half, i, :],
                                                       norm2[:, e.half, 2, i:i + 1], norm2[:, e.half, 4, i:i + 1],
                                                       ALU.add, ALU.mult)
                    last.then_inc(s["out_rest_ready"], 1)

            steps(dve, 0, body, attention_weights)
            dve.wait_ge(s["total_ready"], GROUPS)
            nc.vector.memset(ones_f[:, :], 1.0).then_inc(s_flag, 1)
            nc.vector.tensor_scalar(adj_high[:, :], adj_total[:, :], 0.0, None, ALU.is_gt).then_inc(s_flag, 1)
            dve.wait_ge(s_flag, 3)
            nc.vector.tensor_copy(flag_sb[:, :], ps_t0[0:1, 0, 0:1]).then_inc(s_flag, 1)
            dve.wait_ge(s_flag, 4)
            some = dve.value_load(flag_sb[0:1, 0:1], min_val=0, max_val=N)
            with dve.If(some > 0):
                nc.vector.memset(zeros_f[:, :], 0.0)
                dve.wait_ge(s_dir_pe, 1)
                nc.vector.tensor_copy(whg_dir[:, :, D:2 * D], ps_o[:, 0:2, :]).then_inc(s_dir_dve, 1)
                with dve.Fori(0, B) as b:
                    dve.wait_ge(s_rel_in, 32 * b + 32)
                    nc.vector.tensor_copy(rel_adjf[:, :], rel_adj[:, :]).then_inc(s_rel_dve, 1)
                    dve.wait_ge(s_rel_pe, REL_PE * b + 3)
                    nc.vector.tensor_copy(rel_adjT[:, :], ps_t1[:, 0, :])
                    nc.vector.tensor_copy(rel_hg[:, 0, :], ps_hg[0][:, 0, :])
                    nc.vector.tensor_copy(rel_hg[:, 1, :], ps_hg[1][:, 0, :]).then_inc(s_rel_dve, 1)
                    nc.vector.memset(rel_id[:, :], 1.0).then_inc(s_rel_dve, 1)
                    with dve.Fori(0, RELATIONS) as r:
                        dve.wait_ge(s_rel_dve, REL_DVE * b + 4 * r + 3)
                        nc.vector.tensor_scalar(rel_id[:, :], rel_id[:, :], 1.0, None, ALU.add).then_inc(s_rel_dve, 1)
                        dve.wait_ge(s_rel_rows, 16 * (RELATIONS * b + r) + 16)
                        nc.vector.tensor_tensor(rel_pre[:, :, :], rel_hg[:, :, :], rel_rows[:, :, :], ALU.add)\
                            .then_inc(s_rel_dve, 1)
                        dve.wait_ge(s_rel_dve, REL_DVE * b + 4 * r + 5)
                        dve.wait_ge(s_rel_pe, REL_PE * b + r + 4)
                        nc.vector.tensor_scalar(rel_mask[:, 0, :], rel_adjT[:, :], rel_id[:, :], 0.5,
                                                ALU.is_equal, ALU.mult)
                        nc.vector.tensor_scalar(rel_mask[:, 1, :], rel_adjf[:, :], rel_id[:, :], 0.5,
                                                ALU.is_equal, ALU.mult).then_inc(s_rel_dve, 1)
                        dve.wait_ge(s_rel_act, RELATIONS * b + r + 1)
                        nc.vector.scalar_tensor_tensor(rel_vals[:, :, :], rel_gate[:, :, :], 1.0,
                                                       rel_pre[:, :, 0:D], ALU.add, ALU.mult).then_inc(s_rel_dve, 1)
                    dve.wait_ge(s_rel_pe, REL_PE * (b + 1))
                    wait_reuse(dve, s_rel_store, 16 * b)
                    nc.vector.tensor_copy(rel_out[:, :], ps_o[:, 0, :]).then_inc(s_rel_dve, 1)

                def body_extra(a, b, c, d, e):
                    body(a, b, c, d, e, extra=True)
                steps(dve, GROUPS // RING, body_extra)

        @block.gpsimd
        def _(pool):
            nc.gpsimd.memset(neg_half[:, :], -0.5)
            nc.gpsimd.memset(zero_cols[:, :, :], 0.0)
            nc.gpsimd.memset(adj_total[:, :], 0.0)
            nc.gpsimd.memset(eps_sb[:, :], EPS).then_inc(s_const, 1)
            pool.wait_ge(s_const, 4)

            def body(a, b, c, d, e):
                if c.live:
                    e_cols = wh_sb[:, c.slot, :, D:D + 2]
                    pool.wait_ge(s["wh_copied"], c.done)
                    wait_reuse(pool, s["rows_ready"], e.done)
                    nc.gpsimd.tensor_tensor(parts_sb[:, c.half, 0], e_cols, zero_cols[:, :, :], ALU.add)\
                        .then_inc(s["hi_ready"], 1)
                    pool.wait_ge(s["hi_ready"], c.done)
                    nc.gpsimd.tensor_tensor(rest_sb[:, c.half], e_cols, parts_sb[:, c.half, 0], ALU.subtract)\
                        .then_inc(s["rest_ready"], 1)
                    pool.wait_ge(s["rest_ready"], c.done)
                    nc.gpsimd.tensor_tensor(parts_sb[:, c.half, 1], rest_sb[:, c.half], zero_cols[:, :, :], ALU.add)\
                        .then_inc(s["mid_ready"], 1)
                    pool.wait_ge(s["mid_ready"], c.done)
                    nc.gpsimd.tensor_tensor(parts_sb[:, c.half, 2], rest_sb[:, c.half], parts_sb[:, c.half, 1],
                                            ALU.subtract).then_inc(s["parts_ready"], 1)
                if e.live:
                    pool.wait_ge(s_stored[e.half], e.back(2).stores)
                    pool.wait_ge(s["safesum_ready"], e.done)
                    nc.gpsimd.tensor_tensor(norm2[:, e.half, 0, :], safesum[:, e.half, :], safesum[:, e.half, :], ALU.mult)\
                        .then_inc(s["square_ready"], 1)
                    pool.wait_ge(s["square_ready"], e.done)
                    nc.gpsimd.tensor_tensor(norm2[:, e.half, 1, :], norm2[:, e.half, 0, :], eps_sb[:, :], ALU.mult)\
                        .then_inc(s["eps_ready"], 1)
                    pool.wait_ge(s["eps_ready"], e.done)
                    pool.wait_ge(s["mv2_ready"], e.done)
                    nc.gpsimd.tensor_tensor(norm2[:, e.half, 3, :], mv2[:, e.half, :, 1], norm2[:, e.half, 1, :], ALU.add)\
                        .then_inc(s["var2_ready"], 1)
                    nc.gpsimd.tensor_scalar(norm2[:, e.half, 2, :], mv2[:, e.half, :, 0], -1.0, 1.0, ALU.mult, ALU.mult)\
                        .then_inc(s["negmean2_ready"], 1)
                    pool.wait_ge(s["var2_ready"], e.done)
                    nc.gpsimd.tensor_tensor(norm2[:, e.half, 4, :], norm2[:, e.half, 3, :], neg_half[:, :], ALU.pow)\
                        .then_inc(s["rstd2_ready"], 1)
                if b.live:
                    pool.wait_ge(s["mv1_ready"], b.done)
                    nc.gpsimd.tensor_tensor(norm1[:, b.slot, 0, :], mv1[:, b.half, :, 1], eps_sb[:, :], ALU.add)\
                        .then_inc(s["var1_ready"], 1)
                    pool.wait_ge(s["var1_ready"], b.done)
                    nc.gpsimd.tensor_tensor(norm1[:, b.slot, 1, :], norm1[:, b.slot, 0, :], neg_half[:, :], ALU.pow)\
                        .then_inc(s["rstd1_ready"], 1)
                if a.live:
                    pool.wait_ge(s["over_ready"], a.done)
                    wait_reuse(pool, s["total_ready"], b.done)
                    nc.gpsimd.tensor_tensor(adj_total[:, :], adj_total[:, :], adj_sum[:, a.half:a.half + 1], ALU.add)\
                        .then_inc(s["total_ready"], 1)
                if e.live:
                    pool.wait_ge(s_const, 4)
                    pool.wait_ge(s["rstd2_ready"], e.done)
                    pool.wait_ge(s["negmean2_ready"], e.done)
                    for i in range(G if d.live else SHARED):
                        last = nc.gpsimd.tensor_scalar(out_sb[:, e.half, i, :], z_sb[:, e.half, i, :],
                                                       norm2[:, e.half, 2, i:i + 1], norm2[:, e.half, 4, i:i + 1],
                                                       ALU.add, ALU.mult)
                    last.then_inc(s["out_ready"], 1)

            steps(pool, 0, body)
            pool.wait_ge(s_flag, 4)
            some = pool.value_load(flag_sb[0:1, 0:1], min_val=0, max_val=N)
            with pool.If(some > 0):
                steps(pool, GROUPS // RING, body)


def kernel(x, adj, nodemask, L0_gnn_W_fwd, L0_gnn_W_bwd, L0_gnn_W_loop, L0_gnn_Wg_fwd, L0_gnn_Wg_bwd,
           L0_gnn_Wg_loop, L0_gnn_b_fwd, L0_gnn_b_bwd, L0_gnn_b_loop, L0_gnn_bg_fwd, L0_gnn_bg_bwd,
           L0_gnn_bg_loop, L1_gnn_W, L1_gnn_a):
    import numpy as np
    import concourse.bacc as bacc
    from concourse.bass_utils import run_bass_kernel_spmd

    selectors = np.zeros((PARTS, G, 2, 2, G, N), np.float32)
    for b in range(G):
        for which in range(2):
            selectors[:, b, which, which, b, :] = 1.0
    grouped = np.asarray(x).reshape(GROUPS, G, N, D)
    x_both = np.stack([grouped.transpose(2, 0, 1, 3), grouped.transpose(3, 0, 1, 2)], axis=2)

    identity = np.eye(D, dtype=np.float32)

    def beside(*parts):
        return np.concatenate([np.asarray(t) for t in parts], axis=1)

    def stacked(fwd, bwd):
        return np.stack([np.asarray(fwd), np.asarray(bwd)], axis=1)

    arrays = {
        "x_both": x_both.reshape(128, GROUPS, 2 * G * 128), "adj": np.asarray(adj).transpose(1, 0, 2),
        "loop_weights": beside(L0_gnn_W_loop, np.asarray(L0_gnn_Wg_loop).T, np.asarray(L0_gnn_W_loop).T),
        "loop_biases": beside(L0_gnn_b_loop, L0_gnn_bg_loop),
        "w_dir": stacked(L0_gnn_W_fwd, L0_gnn_W_bwd),
        "wT_dir": stacked(np.asarray(L0_gnn_W_fwd).T, np.asarray(L0_gnn_W_bwd).T),
        "wgT_dir": stacked(np.asarray(L0_gnn_Wg_fwd).T, np.asarray(L0_gnn_Wg_bwd).T),
        "rel_bias": beside(L0_gnn_b_fwd, L0_gnn_bg_fwd, L0_gnn_b_bwd, L0_gnn_bg_bwd),
        "att_weights": beside(identity, identity - np.float32(1.0 / D), L1_gnn_W, np.asarray(L1_gnn_a).reshape(2, D).T,
                              np.asarray(L1_gnn_W).T),
        "selectors": selectors.reshape(TERMS, 2 * G * N),
    }
    arrays = {name: np.ascontiguousarray(a) for name, a in arrays.items()}
    nc = bacc.Bacc("TRN2", target_bir_lowering=False, num_devices=1)
    ins = [nc.dram_tensor(name, a.shape, mybir.dt.from_np(a.dtype), kind="ExternalInput").ap()
           for name, a in arrays.items()]
    out = nc.dram_tensor("out", (N, B, D), F32, kind="ExternalOutput").ap()
    gnn_kernel(nc, *ins, out)
    r = run_bass_kernel_spmd(nc, [arrays], core_ids=[0])
    return np.ascontiguousarray(r.results[0]["out"].transpose(1, 0, 2))
```
